# Optimizing a Trainium2 kernel written in Bass

```python
import numpy as np
import jax
import jax.numpy as jnp

def _softmax(x, axis=-1):
    return jax.nn.softmax(x, axis=axis)

def _gelu(x):
    return jax.nn.gelu(x, approximate=True)

def _silu(x):
    return jax.nn.silu(x)

def _sigmoid(x):
    return jax.nn.sigmoid(x)

def _layernorm(x, axis=-1, eps=1e-05):
    m = jnp.mean(x, axis=axis, keepdims=True)
    v = jnp.var(x, axis=axis, keepdims=True)
    return (x - m) / jnp.sqrt(v + eps)

def _scatter_add(tgt, idx, src, axis=0):
    return tgt.at[idx].add(src)

def _segment_sum(src, seg, n):
    return jax.ops.segment_sum(src, seg, n)
kernel_name = 'mk_seq_preln_d1_jaxref_r8_f59ed2'

def setup_inputs(seed: int=0):
    np.random.seed(seed)
    _w = jnp.asarray

    def _L0_attn_setup():
        import jax, jax.numpy as jnp
        import numpy as np
        NUM_HEADS = 16

        def _stablemax3_s(x):
            pos = 1.0 + x * (1.0 + 0.5 * x * (1.0 + x / 3.0))
            neg = 1.0 / (1.0 - x * (1.0 - 0.5 * x * (1.0 - x / 3.0)))
            return jnp.where(x >= 0, pos, neg)

        def stablemax3(logits, axis=-1):
            logits = logits - jnp.max(logits, axis=axis, keepdims=True)
            s = _stablemax3_s(logits)
            return s / jnp.sum(s, axis=axis, keepdims=True)
        key = jax.random.key(seed)
        k1, k2, k3 = jax.random.split(key, 3)
        B, S, D = (2, 256, 128)
        x = jax.random.normal(k1, (B, S, D), dtype=jnp.float32)
        w_qkv = jax.random.normal(k2, (3 * D, D), dtype=jnp.float32) * 0.02
        w_out = jax.random.normal(k3, (D, D), dtype=jnp.float32) * 0.02
        b_out = jnp.zeros((D,), dtype=jnp.float32)
        return {'x': x, 'w_qkv': w_qkv, 'w_out': w_out, 'b_out': b_out}
    _L0_attn_in = _L0_attn_setup()

    def _L0_ffn_setup():
        import jax, jax.numpy as jnp
        import numpy as np
        B, S, D, F, E, K = (4, 256, 128, 512, 4, 2)
        key = jax.random.key(seed)
        k = jax.random.split(key, 6)
        x = jax.random.normal(k[0], (B, S, D), jnp.float32)
        router_w = jax.random.normal(k[1], (D, E), jnp.float32) * D ** (-0.5)
        router_b = jnp.zeros((E,), jnp.float32)
        w1 = jax.random.normal(k[2], (E, D, F), jnp.float32) * 0.02
        w3 = jax.random.normal(k[3], (E, D, F), jnp.float32) * 0.02
        w2 = jax.random.normal(k[4], (E, F, D), jnp.float32) * 0.02
        return {'x': x, 'router_w': router_w, 'router_b': router_b, 'w1': w1, 'w3': w3, 'w2': w2}
    _L0_ffn_in = _L0_ffn_setup()
    _d = {'L0_attn_x': _L0_attn_in['x'], 'L0_attn_w_qkv': _L0_attn_in['w_qkv'], 'L0_attn_w_out': _L0_attn_in['w_out'], 'L0_attn_b_out': _L0_attn_in['b_out'], 'L0_ffn_router_w': _L0_ffn_in['router_w'], 'L0_ffn_router_b': _L0_ffn_in['router_b'], 'L0_ffn_w1': _L0_ffn_in['w1'], 'L0_ffn_w3': _L0_ffn_in['w3'], 'L0_ffn_w2': _L0_ffn_in['w2']}
    _x0 = _d['L0_attn_x']
    _d['L0_attn_x'] = jax.random.normal(jax.random.fold_in(jax.random.key(seed), 1), (32, 256, 128), dtype=_x0.dtype)
    del _x0
    return _d

def reference(L0_attn_x, L0_attn_w_qkv, L0_attn_w_out, L0_attn_b_out, L0_ffn_router_w, L0_ffn_router_b, L0_ffn_w1, L0_ffn_w3, L0_ffn_w2):

    def _L0_attn_ref(x, w_qkv, w_out, b_out):
        import jax, jax.numpy as jnp
        import numpy as np
        NUM_HEADS = 16

        def _stablemax3_s(x):
            pos = 1.0 + x * (1.0 + 0.5 * x * (1.0 + x / 3.0))
            neg = 1.0 / (1.0 - x * (1.0 - 0.5 * x * (1.0 - x / 3.0)))
            return jnp.where(x >= 0, pos, neg)

        def stablemax3(logits, axis=-1):
            logits = logits - jnp.max(logits, axis=axis, keepdims=True)
            s = _stablemax3_s(logits)
            return s / jnp.sum(s, axis=axis, keepdims=True)
        B, S, D = x.shape
        H = NUM_HEADS
        hd = D // H
        scale = hd ** (-0.5)
        qkv = x @ w_qkv.T
        qkv = qkv.reshape(B, S, 3, H, hd)
        qkv = jnp.transpose(qkv, (2, 0, 3, 1, 4))
        q, k, v = (qkv[0], qkv[1], qkv[2])
        attn = jnp.einsum('bhsd,bhtd->bhst', q, k) * scale
        attn = stablemax3(attn, axis=-1)
        out = jnp.einsum('bhst,bhtd->bhsd', attn, v)
        out = jnp.transpose(out, (0, 2, 1, 3)).reshape(B, S, D)
        return out @ w_out.T + b_out

    def _L0_ffn_ref(x, router_w, router_b, w1, w3, w2):
        import jax, jax.numpy as jnp
        import numpy as np
        B, S, D, F, E, K = (4, 256, 128, 512, 4, 2)
        b, s, d = x.shape
        T = b * s
        e = router_w.shape[1]
        xf = x.reshape(T, d)
        logits = xf @ router_w + router_b
        probs = jax.nn.softmax(logits, axis=-1)
        top_p, top_i = jax.lax.top_k(probs, K)
        top_p = top_p / jnp.sum(top_p, axis=-1, keepdims=True)
        gates = jnp.zeros((T, e), xf.dtype).at[jnp.arange(T)[:, None], top_i].add(top_p)
        h = jax.nn.silu(jnp.einsum('td,edf->etf', xf, w1)) * jnp.einsum('td,edf->etf', xf, w3)
        expert_out = jnp.einsum('etf,efd->etd', h, w2)
        out = jnp.einsum('te,etd->td', gates, expert_out)
        return out.reshape(b, s, d)
    x = L0_attn_x
    x = x + _L0_attn_ref(_layernorm(x, axis=-1), L0_attn_w_qkv, L0_attn_w_out, L0_attn_b_out)
    x = x + _L0_ffn_ref(_layernorm(x, axis=-1), L0_ffn_router_w, L0_ffn_router_b, L0_ffn_w1, L0_ffn_w3, L0_ffn_w2)
    return x

_drawn_inputs = setup_inputs


def setup_inputs(seed=0):
    import zlib

    import numpy as np

    out = dict(_drawn_inputs(seed))
    spreads = {'L0_attn_b_out': (0.0, 0.1), 'L0_ffn_router_b': (0.0, 0.8)}
    factors = {'L0_attn_w_qkv': 8.0,
     'L0_attn_w_out': 8.0,
     'L0_ffn_router_w': 8.0,
     'L0_ffn_w1': 6.373,
     'L0_ffn_w3': 6.343,
     'L0_ffn_w2': 6.352}
    for name, (base, spread) in spreads.items():
        noise = np.random.default_rng([zlib.crc32(name.encode()), seed]).standard_normal(out[name].shape)
        drawn = base * np.exp(spread * noise) if base else spread * noise
        out[name] = jnp.asarray(drawn.astype(out[name].dtype))
    for name, factor in factors.items():
        out[name] = (out[name] * factor).astype(out[name].dtype)
    return out
```

```python
import concourse.bass as bass
from concourse import mybir
from contextlib import ExitStack


def attention_then_experts_kernel(nc: bass.Bass, x: bass.AP, w_qkv: bass.AP, w_out: bass.AP, b_out: bass.AP,
                                  router_w: bass.AP, router_b: bass.AP, w1: bass.AP, w3: bass.AP, w2: bass.AP,
                                  out: bass.AP):
    F32 = mybir.dt.float32
    F32R = mybir.dt.float32r
    ALU = mybir.AluOpType
    ACT = mybir.ActivationFunctionType
    AX = mybir.AxisListType

    B, S, D = x.shape
    E, _, F = w1.shape
    H = 16
    HD = D // H
    SCALE = float(HD) ** -0.5
    EPS = 1e-5
    C = S // 128
    G = H // 4
    FB = F // 128
    NB = E * FB
    U = G * C
    MROW = 96
    KROWS = MROW + 2
    UP = NB // 2

    scratch = nc.dram_tensor("qk_scratch", [4, 128, S], F32).ap()

    def row_to_all(ap, n):
        return bass.AP(ap.tensor, ap.offset, [[0, 128], [1, n]])

    ctx = ExitStack()
    with ctx:
        def sb(name, shape, dt=F32):
            return ctx.enter_context(nc.sbuf_tensor(name, shape, dt))

        def sem(name):
            return ctx.enter_context(nc.semaphore(name))

        ident = sb("ident", [128, 128])
        proj_T = sb("proj_T", [128, 4, D])
        w1_hi = sb("w1_hi", [128, E, F], F32R)
        w1_lo = sb("w1_lo", [128, E, F], F32R)
        w3_hi = sb("w3_hi", [128, E, F], F32R)
        w3_lo = sb("w3_lo", [128, E, F], F32R)
        w2_sb = sb("w2_sb", [128, NB, D])
        rw_raw = sb("rw_raw", [128, E])
        rw_hi = sb("rw_hi", [128, E], F32R)
        rw_lo = sb("rw_lo", [128, E], F32R)
        b_out_all = sb("b_out_all", [128, D])
        router_b_all = sb("router_b_all", [128, E])
        earlier = sb("earlier", [128, E, E])
        x_in = sb("x_in", [128, C, D])
        xn = sb("xn", [128, C, D])
        xn_T = sb("xn_T", [128, S])
        qk_split = sb("qk_split", [128, 4, S], F32R)
        q_stack = [sb(f"q_stack{i}", [128, H, S], F32R) for i in range(2)]
        k_stack = [sb(f"k_stack{i}", [128, H, S], F32R) for i in range(2)]
        v_pad = [sb(f"v_pad{i}", [128, C, H, 32]) for i in range(2)]
        mx = sb("mx", [128, C, H])
        m_split = sb("m_split", [H, 2, S], F32R)
        w_sq = sb("w_sq", [128, 2, 4 * S])
        poly = sb("poly", [128, U, 4 * S])
        o_T = sb("o_T", [128, G, S])
        den_r = sb("den_r", [128, C, H])
        attn = sb("attn", [128, C, D])
        attn_T = sb("attn_T", [128, S])
        x_res = sb("x_res", [128, C, D])
        x_resb = sb("x_resb", [128, C, D])
        y_acc = [sb(f"y_acc{i}", [128, C, D]) for i in range(2)]
        two = sb("two", [128, 1])
        stats = sb("stats", [128, 2 * C, 6])
        mean_var = sb("mean_var", [128, 2 * C, 2])
        eps_all = sb("eps_all", [128, 2 * C])
        minus_half = sb("minus_half", [128, 2 * C])
        three_halves = sb("three_halves", [128, 2 * C])
        half_var = sb("half_var", [128, 2 * C])
        var_eps = sb("var_eps", [128, 2 * C])
        ln_var = sb("ln_var", [128, 2 * C])
        rstd0 = sb("rstd0", [128, 2 * C])
        newton = sb("newton", [128, 2 * C])
        rstd = sb("rstd", [128, 2 * C])
        xn2 = sb("xn2", [128, C, D])
        xn2_hi = sb("xn2_hi", [128, S], F32R)
        xn2_lo = sb("xn2_lo", [128, S], F32R)
        silu_a = sb("silu_a", [128, 2, 2 * S])
        hid = sb("hid", [128, NB, S])
        logits = sb("logits", [128, C, E])
        top_l = sb("top_l", [128, C])
        shifted = sb("shifted", [128, C, E])
        exp_l = sb("exp_l", [128, C, E])
        above = sb("above", [128, C, E, E])
        equal = sb("equal", [128, C, E, E])
        rank = sb("rank", [128, C, E])
        chosen = sb("chosen", [128, C, E])
        chosen_sum = sb("chosen_sum", [128, C])
        chosen_r = sb("chosen_r", [128, C])
        gates = [sb(f"gates{i}", [128, C, E]) for i in range(2)]

        sc = ctx.enter_context(nc.psum_tensor("sc", [128, 2, 4 * S], F32))
        up_a = ctx.enter_context(nc.psum_tensor("up_a", [128, 2 * S], F32))
        up_b = ctx.enter_context(nc.psum_tensor("up_b", [128, 2 * S], F32))
        pv = ctx.enter_context(nc.psum_tensor("pv", [128, 2, S], F32))
        misc = ctx.enter_context(nc.psum_tensor("misc", [128, 512], F32))

        ld_w = sem("ld_w")
        ident_ok = sem("ident_ok")
        consts_ok = sem("consts_ok")
        consts_v = sem("consts_v")
        q_blank = sem("q_blank")
        k_blank = sem("k_blank")
        split_ok = sem("split_ok")
        wT_full = sem("wT_full")
        proj_ok = sem("proj_ok")
        x_loaded = sem("x_loaded")
        xr_loaded = sem("xr_loaded")
        xres_ok = sem("xres_ok")
        agg_ok = sem("agg_ok")
        var_ok = sem("var_ok")
        lnv_ok = sem("lnv_ok")
        rstd0_ok = sem("rstd0_ok")
        newton_step = sem("newton_step")
        rstd_ok = sem("rstd_ok")
        xn_ok = sem("xn_ok")
        xn2_ok = sem("xn2_ok")
        xnT_full = sem("xnT_full")
        xnT_ok = sem("xnT_ok")
        qk_full = sem("qk_full")
        qk_hi_ok = sem("qk_hi_ok")
        qk_ok = sem("qk_ok")
        v_full = sem("v_full")
        v_ok = sem("v_ok")
        qk_stored = sem("qk_stored")
        stacked = [sem(f"stacked{i}") for i in range(2)]
        s_full = sem("s_full")
        s_used = sem("s_used")
        mT_full = sem("mT_full")
        m_hi_ok = sem("m_hi_ok")
        m_ok = sem("m_ok")
        m_stacked = [sem(f"m_stacked{i}") for i in range(2)]
        w_full = sem("w_full")
        sq_ok = sem("sq_ok")
        poly_ok = sem("poly_ok")
        ln_ok = sem("ln_ok")
        p_ok = sem("p_ok")
        pv_full = sem("pv_full")
        o_ok0 = sem("o_ok0")
        o_ok1 = sem("o_ok1")
        oq_full = sem("oq_full")
        den_ok = sem("den_ok")
        attn_ok = sem("attn_ok")
        attnT_full = sem("attnT_full")
        attnT_ok = sem("attnT_ok")
        res_full = sem("res_full")
        y_ok = sem("y_ok")
        xn2T_full = sem("xn2T_full")
        xn2_hi_ok = sem("xn2_hi_ok")
        xn2_lo_ok = sem("xn2_lo_ok")
        lg_full = sem("lg_full")
        lg_ok = sem("lg_ok")
        shift_ok = sem("shift_ok")
        exp_ok = sem("exp_ok")
        route_step = sem("route_step")
        gates_ok = sem("gates_ok")
        a_full = sem("a_full")
        silu_ok = sem("silu_ok")
        b_full = sem("b_full")
        hid_ok = sem("hid_ok")
        down_full = sem("down_full")
        acc_ok = sem("acc_ok")
        stored = [sem(f"stored{i}") for i in range(2)]

        ROUTE = 6

        def no(i, off):
            return 2 * i + off

        def has(i, off):
            return not isinstance(i, int) or 0 <= no(i, off) < B

        def after(eng, s, count):
            if not isinstance(count, int) or count > 0:
                eng.wait_ge(s, count)

        def pair_count(i, off, each):
            return (i + off // 2 + 1) * each

        def over_batches(eng, half_a, half_b):
            for n in range(-2, 2):
                half_a(n // 2, n % 2)
                half_b(n // 2, n % 2)
            with eng.Fori(1, B // 2 - 1) as i:
                for off in range(2):
                    half_a(i, off)
                    half_b(i, off)
            for n in range(B - 2, B + 2):
                half_a(n // 2, n % 2)
                half_b(n // 2, n % 2)

        block = ctx.enter_context(nc.Block())

        @block.sync
        def _(sp):
            sp.dma_start(poly[:, 4, 0:3 * D].rearrange("p (s d) -> p s d", s=3),
                         w_qkv.rearrange("(s o) d -> o s d", s=3)).then_inc(ld_w, 16)
            sp.dma_start(poly[:, 4, 3 * D:4 * D], w_out).then_inc(ld_w, 16)
            sp.dma_start(b_out_all[:], row_to_all(b_out, D)).then_inc(ld_w, 16)
            sp.dma_start(router_b_all[:], row_to_all(router_b, E)).then_inc(ld_w, 16)
            sp.dma_start(rw_raw[:], router_w).then_inc(ld_w, 16)
            sp.dma_start(poly[:, 0:2, :].rearrange("p a (b f) -> p (a b) f", b=2),
                         w1.rearrange("e d f -> d e f")).then_inc(ld_w, 16)
            sp.dma_start(poly[:, 2:4, :].rearrange("p a (b f) -> p (a b) f", b=2),
                         w3.rearrange("e d f -> d e f")).then_inc(ld_w, 16)
            sp.dma_start(w2_sb[:], w2.rearrange("e (c p) d -> p (e c) d", p=128)).then_inc(ld_w, 16)

            def value(v):
                if not isinstance(v, int):
                    sp.compute_val(v)
                return v

            def address(offset):
                value(offset)
                value(offset * 4)
                return offset

            def batch_at(t, offset):
                return bass.AP(t.tensor, offset, [[D, 128], [128 * D, C], [1, D]])

            def first_half(i, off):
                n = no(i, off)
                par = (off + 1) % 2
                xn_used, x_from, y_from = value(n + 2), address((n + 2) * S * D), address(n * S * D)
                split, scratch_read, w_used = value(n + 2), value(pair_count(i, off, 128)), value(U * n)
                stored_qk, res_used = value(16 * (n + 2)), value(n)
                if has(i, off + 2):
                    after(sp, xn_ok, xn_used)
                    sp.dma_start(x_in[:], batch_at(x, x_from)).then_inc(x_loaded, 16)
                if has(i, off + 1):
                    after(sp, qk_ok, split)
                    after(sp, stacked[1 - par], scratch_read)
                    sp.dma_start(scratch.rearrange("a p t -> p a t"), qk_split[:].bitcast(F32)).then_inc(qk_stored, 16)
                    after(sp, w_full, w_used)
                    sp.wait_ge(qk_stored, stored_qk)
                    if isinstance(i, int) and 0 <= n + 1 < 2:
                        sp.wait_ge(q_blank, n + 2)
                        sp.wait_ge(k_blank, 2 * (n + 2))
                    for stack, parts in ((q_stack, (0, 0, 1, 1)), (k_stack, (2, 3, 2, 3))):
                        for r, part in enumerate(parts):
                            sp.dma_start(stack[par][HD * r:HD * (r + 1), :, :].bitcast(F32),
                                         scratch[part].rearrange("(h d) t -> d h t", d=HD)).then_inc(stacked[par], 16)
                if has(i, off):
                    after(sp, xres_ok, res_used)
                    sp.dma_start(x_res[:], batch_at(x, y_from)).then_inc(xr_loaded, 16)

            def second_half(i, off):
                n = no(i, off)
                m_split_at, added, out_at = value(n + 2), value(E * C * (n - 1)), address((n - 2) * S * D)
                if has(i, off + 1):
                    par = (off + 1) % 2
                    sp.wait_ge(m_ok, m_split_at)
                    for a in range(2):
                        sp.dma_start(q_stack[par][MROW + a:MROW + a + 1, :, :].bitcast(F32),
                                     m_split[:, a, :].bitcast(F32)).then_inc(m_stacked[par], 16)
                if has(i, off - 2):
                    par = off % 2
                    sp.wait_ge(acc_ok, added)
                    sp.dma_start(batch_at(out, out_at), y_acc[par][:]).then_inc(stored[par], 16)

            over_batches(sp, first_half, second_half)
            for par in range(2):
                sp.wait_ge(stored[par], 16 * (B // 2))

        @block.gpsimd
        def _(pool):
            nc.gpsimd.memset(ident[:], 0.0).then_inc(consts_ok, 1)
            nc.gpsimd.memset(earlier[:], 1.0).then_inc(consts_ok, 1)
            nc.gpsimd.memset(eps_all[:], EPS)
            nc.gpsimd.memset(minus_half[:], -0.5)
            nc.gpsimd.memset(three_halves[:], 1.5).then_inc(consts_ok, 1)
            pool.wait_ge(consts_ok, 3)
            nc.gpsimd.affine_select(out=ident[:], in_=ident[:], compare_op=ALU.not_equal, fill=1.0, base=0,
                                    pattern=[[-1, 128]], channel_multiplier=1).then_inc(ident_ok, 1)
            nc.gpsimd.affine_select(out=earlier[:], in_=earlier[:], compare_op=ALU.is_ge, fill=0.0, base=-1,
                                    pattern=[[1, E], [-1, E]], channel_multiplier=0).then_inc(consts_ok, 1)
            pool.wait_ge(consts_ok, 4)
            for par in range(2):
                nc.gpsimd.memset(k_stack[par][0:MROW].bitcast(F32), 0.0).then_inc(k_blank, 1)
                pool.wait_ge(k_blank, 2 * par + 1)
                nc.gpsimd.memset(k_stack[par][MROW:KROWS].bitcast(F32), 1.0).then_inc(k_blank, 1)
                pool.wait_ge(k_blank, 2 * par + 2)
            pool.wait_ge(ld_w, 16 * 8)

            def first_half(i, off):
                if has(i, off):
                    m = no(i, off)
                    pool.wait_ge(xr_loaded, 16 * (m + 1))
                    after(pool, y_ok, C * m)
                    for c in range(C):
                        last = nc.gpsimd.tensor_tensor(x_resb[:, c, :], x_res[:, c, :], b_out_all[:], ALU.add)
                    last.then_inc(xres_ok, 1)

            def second_half(i, off):
                lo, hi = (0 if has(i, off - 1) else C), (2 * C if has(i, off + 2) else C)
                if lo < hi:
                    k = no(i, off) + 2
                    s = slice(lo, hi)
                    pool.wait_ge(agg_ok, k + 1)
                    nc.gpsimd.tensor_tensor(var_eps[:, s], mean_var[:, s, 1], eps_all[:, s], ALU.add).then_inc(var_ok, 1)
                    pool.wait_ge(var_ok, k + 1)
                    nc.gpsimd.tensor_tensor(half_var[:, s], var_eps[:, s], minus_half[:, s],
                                            ALU.mult).then_inc(newton_step, 1)
                    pool.wait_ge(rstd0_ok, k + 1)
                    nc.gpsimd.tensor_tensor(newton[:, s], rstd0[:, s], rstd0[:, s], ALU.mult).then_inc(newton_step, 1)
                    pool.wait_ge(newton_step, 4 * k + 2)
                    nc.gpsimd.tensor_tensor(newton[:, s], newton[:, s], half_var[:, s], ALU.mult).then_inc(newton_step, 1)
                    pool.wait_ge(newton_step, 4 * k + 3)
                    nc.gpsimd.tensor_tensor(newton[:, s], newton[:, s], three_halves[:, s],
                                            ALU.add).then_inc(newton_step, 1)
                    pool.wait_ge(newton_step, 4 * k + 4)
                    nc.gpsimd.tensor_tensor(rstd[:, s], rstd0[:, s], newton[:, s], ALU.mult).then_inc(rstd_ok, 1)

            over_batches(pool, first_half, second_half)

        @block.scalar
        def _(act):
            def first_half(i, off):
                n = no(i, off)
                if has(i, off - 1):
                    act.wait_ge(pv_full, G * n)
                    after(act, oq_full, C * (n - 1))
                    nc.scalar.copy(o_T[:, 2:4, :], pv[:]).then_inc(o_ok1, 1)
                if has(i, off + 1):
                    m = n + 1
                    act.wait_ge(xnT_full, m + 1)
                    after(act, v_full, m)
                    nc.scalar.copy(xn_T[:], misc[:, 0:S]).then_inc(xnT_ok, 1)
                for u in range(U):
                    if has(i, off - 2):
                        k = UP * (n - 2) + u
                        act.wait_ge(a_full, k + 1)
                        after(act, hid_ok, k - 1 if u > 1 else k - u)
                        nc.scalar.activation(silu_a[:, u % 2, :], up_a[:], ACT.Silu).then_inc(silu_ok, 1)
                    if has(i, off):
                        k = U * n + u
                        act.wait_ge(w_full, k + 1)
                        after(act, poly_ok, k - 1 if u > 1 else k - u)
                        nc.scalar.activation(w_sq[:, u % 2, :], sc[:, u % 2, :], ACT.Square).then_inc(sq_ok, 1)
                    if u == 0 and has(i, off + 1):
                        m = n + 1
                        act.wait_ge(qk_full, m + 1)
                        after(act, qk_stored, 16 * m)
                        nc.scalar.copy(qk_split[:, 0, :], misc[:, 0:S])
                        nc.scalar.mul(qk_split[:, 2, :], misc[:, S:2 * S], -SCALE).then_inc(qk_hi_ok, 1)
                    if u == 1 and has(i, off + 1):
                        m, par = n + 1, (off + 1) % 2
                        act.wait_ge(v_full, m + 1)
                        act.wait_ge(consts_v, 4)
                        after(act, pv_full, G * (m - 1))
                        for c in range(C):
                            last = nc.scalar.copy(v_pad[par][:, c, :, 0:HD],
                                                  misc[:, c * D:(c + 1) * D].rearrange("p (h d) -> p h d", d=HD))
                        last.then_inc(v_ok, 1)
                    if u == 5 and has(i, off - 1):
                        m = n - 1
                        act.wait_ge(attnT_full, m + 1)
                        after(act, res_full, m)
                        nc.scalar.copy(attn_T[:], misc[:, 0:S]).then_inc(attnT_ok, 1)

            def second_half(i, off):
                n = no(i, off)
                lo, hi = (0 if has(i, off - 1) else C), (2 * C if has(i, off + 2) else C)
                if lo < hi:
                    k = n + 2
                    s = slice(lo, hi)
                    act.wait_ge(var_ok, k + 1)
                    nc.scalar.activation(ln_var[:, s], var_eps[:, s], ACT.Ln).then_inc(lnv_ok, 1)
                    act.wait_ge(lnv_ok, k + 1)
                    after(act, rstd_ok, k)
                    nc.scalar.activation(rstd0[:, s], ln_var[:, s], ACT.Exp, scale=-0.5).then_inc(rstd0_ok, 1)

                def log_of(g):
                    act.wait_ge(poly_ok, U * n + C * (g + 1))
                    nc.scalar.activation(poly[:, C * g:C * (g + 1), :], poly[:, C * g:C * (g + 1), :], ACT.Ln,
                                         bias=two[:]).then_inc(ln_ok, 1)

                def weights_of(g):
                    act.wait_ge(ln_ok, G * n + g + 1)
                    nc.scalar.activation(poly[:, C * g:C * (g + 1), :], poly[:, C * g:C * (g + 1), :], ACT.Exp,
                                         scale=-1.0).then_inc(p_ok, 1)

                if has(i, off):
                    log_of(0)
                for g in range(G):
                    if has(i, off):
                        if g + 1 < G:
                            log_of(g + 1)
                        weights_of(g)
                    if g == 0 and has(i, off - 1):
                        m = n - 1
                        act.wait_ge(xn2T_full, m + 1)
                        after(act, b_full, UP * m)
                        after(act, lg_full, m)
                        nc.scalar.copy(xn2_hi[:], misc[:, 0:S]).then_inc(xn2_hi_ok, 1)
                    if g == 2 and has(i, off - 1):
                        m = n - 1
                        act.wait_ge(shift_ok, m + 1)
                        nc.scalar.activation(exp_l[:], shifted[:], ACT.Exp).then_inc(exp_ok, 1)

            act.wait_ge(consts_v, 4)
            over_batches(act, first_half, second_half)

        @block.vector
        def _(dve):
            nc.vector.memset(two[:], 2.0).then_inc(consts_v, 1)
            for par in range(2):
                nc.vector.memset(q_stack[par][0:MROW].bitcast(F32), 0.0).then_inc(q_blank, 1)
            for par in range(2):
                nc.vector.memset(v_pad[par][:], 0.0)
            nc.vector.memset(gates[0][:], 0.0).then_inc(consts_v, 1)
            dve.wait_ge(consts_v, 2)
            for par in range(2):
                nc.vector.memset(v_pad[par][:, :, :, HD], 1.0).then_inc(consts_v, 1)
            dve.wait_ge(wT_full, 1)
            nc.vector.tensor_copy(proj_T[:].rearrange("p s d -> p (s d)"), misc[:]).then_inc(proj_ok, 1)
            dve.wait_ge(ld_w, 16 * 8)
            raw1 = poly[:, 0:2, :].rearrange("p a n -> p (a n)")
            raw3 = poly[:, 2:4, :].rearrange("p a n -> p (a n)")
            splits = ((w1_hi[:].rearrange("p e f -> p (e f)"), w1_lo[:].rearrange("p e f -> p (e f)"), raw1),
                      (w3_hi[:].rearrange("p e f -> p (e f)"), w3_lo[:].rearrange("p e f -> p (e f)"), raw3),
                      (rw_hi[:], rw_lo[:], rw_raw[:]))
            for k, (hi, lo, raw) in enumerate(splits):
                nc.vector.tensor_copy(hi, raw).then_inc(split_ok, 1)
                dve.wait_ge(split_ok, 2 * k + 1)
                nc.vector.tensor_tensor(lo, raw, hi.bitcast(F32), ALU.subtract).then_inc(split_ok, 1)

            def first_half(i, off):
                n = no(i, off)
                for u in range(U):
                    if has(i, off):
                        k = U * n + u
                        dve.wait_ge(sq_ok, k + 1)
                        if u % C == 0:
                            after(dve, pv_full, G * (n - 1) + u // C + 1)
                        nc.vector.scalar_tensor_tensor(poly[:, u, :], w_sq[:, u % 2, :], 3.0, sc[:, u % 2, :],
                                                       ALU.add, ALU.mult).then_inc(poly_ok, 1)
                    if has(i, off - 2):
                        k = UP * (n - 2) + u
                        dve.wait_ge(b_full, k + 1)
                        dve.wait_ge(silu_ok, k + 1)
                        if u == 0:
                            after(dve, down_full, E * (n - 2))
                        nc.vector.tensor_tensor(hid[:, 2 * u:2 * u + 2, :].rearrange("p a t -> p (a t)"),
                                                silu_a[:, u % 2, :], up_b[:], ALU.mult).then_inc(hid_ok, 1)
                    if u == 0 and has(i, off + 1):
                        m = n + 1
                        dve.wait_ge(qk_hi_ok, m + 1)
                        nc.vector.tensor_tensor(qk_split[:, 1, :], misc[:, 0:S], qk_split[:, 0, :].bitcast(F32),
                                                ALU.subtract)
                        nc.vector.scalar_tensor_tensor(qk_split[:, 3, :], misc[:, S:2 * S], -SCALE,
                                                       qk_split[:, 2, :].bitcast(F32), ALU.mult,
                                                       ALU.subtract).then_inc(qk_ok, 1)
                    if u in (2, 3) and has(i, off - 1):
                        m, c = n - 1, u - 2
                        by_head = misc[:].rearrange("p (h e) -> p h e", e=32)
                        dve.wait_ge(oq_full, C * m + c + 1)
                        nc.vector.reciprocal(den_r[:, c, :], by_head[:, :, HD]).then_inc(den_ok, 1)
                        dve.wait_ge(den_ok, C * m + c + 1)
                        after(dve, attnT_full, m)
                        nc.vector.tensor_tensor(attn[:, c, :].rearrange("p (h d) -> p h d", d=HD),
                                                by_head[:, :, 0:HD],
                                                den_r[:, c, :].unsqueeze(2).to_broadcast([128, H, HD]),
                                                ALU.mult).then_inc(attn_ok, 1)
                    if u == 6 and has(i, off - 1):
                        m, par = n - 1, (off - 1) % 2
                        dve.wait_ge(res_full, m + 1)
                        dve.wait_ge(xres_ok, m + 1)
                        after(dve, stored[par], pair_count(i, off - 3, 16))
                        for c in range(C):
                            nc.vector.tensor_tensor(y_acc[par][:, c, :], misc[:, c * D:(c + 1) * D],
                                                    x_resb[:, c, :], ALU.add).then_inc(y_ok, 1)

            def second_half(i, off):
                n = no(i, off)
                lo, hi = (0 if has(i, off - 1) else C), (2 * C if has(i, off + 2) else C)
                k = n + 2
                if lo < hi:
                    if has(i, off + 2):
                        dve.wait_ge(x_loaded, 16 * (n + 3))
                    if has(i, off - 1):
                        dve.wait_ge(y_ok, C * n)
                    after(dve, rstd_ok, k)
                    for s in range(lo, hi):
                        src = y_acc[(off - 1) % 2][:, s, :] if s < C else x_in[:, s - C, :]
                        nc.vector.bn_stats(stats[:, s, :], src)
                    nc.vector.drain()
                    for s in range(lo, hi):
                        last = nc.vector.bn_aggr(mean_var[:, s, :], stats[:, s, :])
                    last.then_inc(agg_ok, 1)

                def scores_max(u):
                    g, c = u // C, u % C
                    dve.wait_ge(s_full, U * (n + 1) + u + 1)
                    if u == 0:
                        after(dve, mT_full, n + 1)
                    nc.vector.tensor_reduce(mx[:, c, 4 * g:4 * g + 4],
                                            sc[:, u % 2, :].rearrange("p (j t) -> p j t", j=4), AX.X, ALU.min,
                                            negate=True).then_inc(s_used, 1)

                def normalise():
                    dve.wait_ge(rstd_ok, k + 1)
                    for s in range(lo, hi):
                        if s == 0:
                            after(dve, xn2T_full, n - 1)
                        if s == C:
                            after(dve, xnT_full, n + 2)
                        dst, src = ((xn2[:, s, :], y_acc[(off - 1) % 2][:, s, :]) if s < C
                                    else (xn[:, s - C, :], x_in[:, s - C, :]))
                        ins = nc.vector.tensor_scalar(dst, src, mean_var[:, s, 0:1], rstd[:, s:s + 1], ALU.subtract,
                                                      ALU.mult)
                        if s == C - 1:
                            ins.then_inc(xn2_ok, 1)
                        if s == 2 * C - 1:
                            ins.then_inc(xn_ok, 1)

                def add_expert(e):
                    m, par = n - 2, off % 2
                    dve.wait_ge(down_full, E * m + e + 1)
                    bank = (up_a, up_b)[e % 2]
                    for c in range(C):
                        after(dve, acc_ok, E * C * m + C * e - (C - 1) + c if e else 0)
                        nc.vector.scalar_tensor_tensor(y_acc[par][:, c, :], bank[:, c * D:(c + 1) * D],
                                                       gates[par][:, c, e:e + 1], y_acc[par][:, c, :], ALU.mult,
                                                       ALU.add).then_inc(acc_ok, 1)

                def route_logits():
                    m = n - 1
                    dve.wait_ge(lg_full, m + 1)
                    for c in range(C):
                        last = nc.vector.tensor_tensor(logits[:, c, :], misc[:, c * E:(c + 1) * E], router_b_all[:],
                                                       ALU.add)
                    last.then_inc(lg_ok, 1)
                    dve.wait_ge(lg_ok, m + 1)
                    nc.vector.tensor_reduce(top_l[:], logits[:], AX.X, ALU.max).then_inc(route_step, 1)
                    dve.wait_ge(route_step, ROUTE * m + 1)
                    after(dve, exp_ok, m)
                    nc.vector.tensor_tensor(shifted[:], logits[:], top_l[:].unsqueeze(2).to_broadcast([128, C, E]),
                                            ALU.subtract).then_inc(shift_ok, 1)
                    for c in range(C):
                        l_j = logits[:, c, :].unsqueeze(1).to_broadcast([128, E, E])
                        l_i = logits[:, c, :].unsqueeze(2).to_broadcast([128, E, E])
                        nc.vector.tensor_tensor(above[:, c], l_j, l_i, ALU.is_gt)
                        last = nc.vector.tensor_tensor(equal[:, c], l_j, l_i, ALU.is_equal)
                    last.then_inc(route_step, 1)
                    dve.wait_ge(route_step, ROUTE * m + 2)
                    for c in range(C):
                        last = nc.vector.tensor_tensor(equal[:, c], equal[:, c], earlier[:], ALU.mult)
                    last.then_inc(route_step, 1)
                    dve.wait_ge(route_step, ROUTE * m + 3)
                    nc.vector.tensor_tensor(above[:].rearrange("p c i j -> p (c i j)"),
                                            above[:].rearrange("p c i j -> p (c i j)"),
                                            equal[:].rearrange("p c i j -> p (c i j)"), ALU.add).then_inc(route_step, 1)
                    dve.wait_ge(route_step, ROUTE * m + 4)
                    nc.vector.tensor_reduce(rank[:], above[:], AX.X, ALU.add).then_inc(route_step, 1)

                def route_gates():
                    m, par = n - 1, (off - 1) % 2
                    dve.wait_ge(route_step, ROUTE * m + 5)
                    dve.wait_ge(exp_ok, m + 1)
                    nc.vector.scalar_tensor_tensor(chosen[:], rank[:], 1.5, exp_l[:], ALU.is_lt,
                                                   ALU.mult).then_inc(gates_ok, 1)
                    dve.wait_ge(gates_ok, 3 * m + 1)
                    nc.vector.tensor_reduce(chosen_sum[:], chosen[:], AX.X, ALU.add).then_inc(gates_ok, 1)
                    dve.wait_ge(gates_ok, 3 * m + 2)
                    nc.vector.reciprocal(chosen_r[:], chosen_sum[:]).then_inc(gates_ok, 1)
                    dve.wait_ge(gates_ok, 3 * m + 3)
                    nc.vector.tensor_tensor(gates[par][:], chosen[:],
                                            chosen_r[:].unsqueeze(2).to_broadcast([128, C, E]),
                                            ALU.mult).then_inc(route_step, 1)

                for u in range(U):
                    if has(i, off + 1):
                        scores_max(u)
                    if u == 1 and lo < hi:
                        normalise()
                    if u % 2 == 1 and u < U - 1 and has(i, off - 2):
                        if u == 1:
                            after(dve, route_step, ROUTE * (n - 1))
                        add_expert(u // 2)
                    if u == 4 and has(i, off - 1):
                        m = n - 1
                        dve.wait_ge(xn2_hi_ok, m + 1)
                        nc.vector.tensor_tensor(xn2_lo[:], misc[:, 0:S], xn2_hi[:].bitcast(F32),
                                                ALU.subtract).then_inc(xn2_lo_ok, 1)
                if has(i, off - 1):
                    route_logits()
                if has(i, off + 1):
                    m = n + 1
                    dve.wait_ge(mT_full, m + 1)
                    after(dve, m_stacked[off % 2], pair_count(i, off, 32))
                    nc.vector.tensor_scalar(m_split[:, 0, :], misc[0:H, 0:S], 1.0, None, ALU.add).then_inc(m_hi_ok, 1)
                    dve.wait_ge(m_hi_ok, m + 1)
                    nc.vector.scalar_tensor_tensor(m_split[:, 1, :], misc[0:H, 0:S], 1.0,
                                                   m_split[:, 0, :].bitcast(F32), ALU.add,
                                                   ALU.subtract).then_inc(m_ok, 1)
                if has(i, off):
                    dve.wait_ge(pv_full, G * n + 2)
                    after(dve, oq_full, C * n)
                    nc.vector.tensor_copy(o_T[:, 0:2, :], pv[:]).then_inc(o_ok0, 1)
                if has(i, off - 2):
                    add_expert(E - 1)
                if has(i, off - 1):
                    route_gates()

            dve.wait_ge(consts_ok, 4)
            over_batches(dve, first_half, second_half)

        @block.tensor
        def _(pe):
            pe.wait_ge(ident_ok, 1)
            pe.wait_ge(ld_w, 16 * 8)
            for s in range(4):
                last = nc.tensor.transpose(misc[:, s * D:(s + 1) * D], poly[:, 4, s * D:(s + 1) * D], ident[:])
            last.then_inc(wT_full, 1)
            pe.wait_ge(proj_ok, 1)
            pe.wait_ge(split_ok, 6)
            pe.wait_ge(k_blank, 4)
            pe.wait_ge(q_blank, 2)

            def exact(dst, lhs, rhs):
                terms = ((0, 0), (0, 1), (1, 0))
                for k, (a, b) in enumerate(terms):
                    last = nc.tensor.matmul(dst, lhs[a], rhs[b], start=(k == 0), stop=(k == len(terms) - 1))
                return last

            def first_half(i, off):
                n = no(i, off)
                if has(i, off + 1):
                    m = n + 1
                    pe.wait_ge(xn_ok, m + 1)
                    after(pe, m_ok, m)
                    for c in range(C):
                        last = nc.tensor.transpose(misc[:, c * 128:(c + 1) * 128], xn[:, c, :], ident[:])
                    last.then_inc(xnT_full, 1)
                for u in range(U):
                    if has(i, off - 2):
                        m = n - 2
                        k = UP * m + u
                        after(pe, silu_ok, k)
                        if u == 0:
                            after(pe, acc_ok, E * C * m)
                            pe.wait_ge(xn2_lo_ok, m + 1)
                        for half in range(2):
                            e, f = divmod(2 * u + half, FB)
                            fs = slice(f * 128, (f + 1) * 128)
                            last = exact(up_a[:, half * S:(half + 1) * S], (w1_hi[:, e, fs], w1_lo[:, e, fs]),
                                         (xn2_hi[:], xn2_lo[:]))
                        last.then_inc(a_full, 1)
                    if has(i, off):
                        par = off % 2
                        k = U * n + u
                        g, c = u // C, u % C
                        if u < 2:
                            pe.wait_ge(s_used, U * (n + 1) - 1 + u)
                        else:
                            pe.wait_ge(poly_ok, k - 1)
                        if u == 0:
                            pe.wait_ge(m_stacked[par], pair_count(i, off, 32))
                        for j in range(4):
                            last = nc.tensor.matmul(sc[:, u % 2, j * S:(j + 1) * S],
                                                    k_stack[par][0:KROWS, 4 * g + j, c * 128:(c + 1) * 128],
                                                    q_stack[par][0:KROWS, 4 * g + j, :], start=True, stop=True)
                        last.then_inc(w_full, 1)
                    if has(i, off - 2):
                        m = n - 2
                        k = UP * m + u
                        after(pe, hid_ok, k)
                        for half in range(2):
                            e, f = divmod(2 * u + half, FB)
                            fs = slice(f * 128, (f + 1) * 128)
                            last = exact(up_b[:, half * S:(half + 1) * S], (w3_hi[:, e, fs], w3_lo[:, e, fs]),
                                         (xn2_hi[:], xn2_lo[:]))
                        last.then_inc(b_full, 1)
                    if u == 0 and has(i, off + 1):
                        m = n + 1
                        pe.wait_ge(xnT_ok, m + 1)
                        nc.tensor.matmul(misc[:, 0:S], proj_T[:, 0, :], xn_T[:], start=True, stop=True)
                        nc.tensor.matmul(misc[:, S:2 * S], proj_T[:, 1, :], xn_T[:], start=True,
                                         stop=True).then_inc(qk_full, 1)
                    if u == 1 and has(i, off + 1):
                        m = n + 1
                        pe.wait_ge(qk_ok, m + 1)
                        for c in range(C):
                            last = nc.tensor.matmul(misc[:, c * D:(c + 1) * D], xn_T[:, c * 128:(c + 1) * 128],
                                                    proj_T[:, 2, :], start=True, stop=True)
                        last.then_inc(v_full, 1)
                    if u in (2, 3) and has(i, off - 1):
                        m, c = n - 1, u - 2
                        if c == 0:
                            pe.wait_ge(o_ok1, m + 1)
                            pe.wait_ge(o_ok0, m + 1)
                            if has(i, off + 1):
                                pe.wait_ge(v_ok, n + 2)
                            else:
                                pe.wait_ge(lg_ok, m)
                        else:
                            pe.wait_ge(attn_ok, C * m + c)
                        for g in range(G):
                            last = nc.tensor.transpose(misc[:, g * 128:(g + 1) * 128],
                                                       o_T[:, g, c * 128:(c + 1) * 128], ident[:])
                        last.then_inc(oq_full, 1)
                    if u == 4 and has(i, off - 1):
                        m = n - 1
                        pe.wait_ge(attn_ok, C * (m + 1))
                        for c in range(C):
                            last = nc.tensor.transpose(misc[:, c * 128:(c + 1) * 128], attn[:, c, :], ident[:])
                        last.then_inc(attnT_full, 1)
                    if u == 5 and has(i, off - 1):
                        m = n - 1
                        pe.wait_ge(attnT_ok, m + 1)
                        for c in range(C):
                            last = nc.tensor.matmul(misc[:, c * D:(c + 1) * D], attn_T[:, c * 128:(c + 1) * 128],
                                                    proj_T[:, 3, :], start=True, stop=True)
                        last.then_inc(res_full, 1)

            def second_half(i, off):
                n = no(i, off)

                def scores(u):
                    m, par = n + 1, (off + 1) % 2
                    g, c = u // C, u % C
                    if u < 2:
                        after(pe, poly_ok, U * m - 1 + u)
                        if u == 0:
                            pe.wait_ge(stacked[par], pair_count(i, off + 1, 128))
                    else:
                        pe.wait_ge(s_used, U * m + u - 1)
                    for j in range(4):
                        last = nc.tensor.matmul(sc[:, u % 2, j * S:(j + 1) * S],
                                                q_stack[par][0:MROW, 4 * g + j, c * 128:(c + 1) * 128],
                                                k_stack[par][0:MROW, 4 * g + j, :], start=True, stop=True)
                    last.then_inc(s_full, 1)

                def down(e):
                    m = n - 2
                    bank = (up_a, up_b)[e % 2]
                    if e == 0:
                        pe.wait_ge(hid_ok, UP * (m + 1))
                    if e >= 2:
                        pe.wait_ge(acc_ok, E * C * m + C * (e - 1))
                    for c in range(C):
                        for f in range(FB):
                            last = nc.tensor.matmul(bank[:, c * D:(c + 1) * D], hid[:, FB * e + f, c * 128:(c + 1) * 128],
                                                    w2_sb[:, FB * e + f, :], start=(f == 0), stop=(f == FB - 1))
                    last.then_inc(down_full, 1)

                def weighted_values(g):
                    par = off % 2
                    pe.wait_ge(p_ok, G * n + g + 1)
                    if g == 0:
                        pe.wait_ge(v_ok, n + 1)
                        after(pe, o_ok1, n)
                    if g == 2:
                        pe.wait_ge(o_ok0, n + 1)
                    for c in range(C):
                        for j in range(4):
                            last = nc.tensor.matmul(pv[32 * j:32 * j + 32, g % 2, :], v_pad[par][:, c, 4 * g + j, :],
                                                    poly[:, C * g + c, j * S:(j + 1) * S], start=(c == 0),
                                                    stop=(c == C - 1))
                    last.then_inc(pv_full, 1)

                for u in range(U):
                    if has(i, off + 1):
                        scores(u)
                    if u % 2 == 0 and has(i, off - 2):
                        down(u // 2)
                    if u == 2 and has(i, off - 1):
                        m = n - 1
                        pe.wait_ge(xn2_ok, m + 1)
                        pe.wait_ge(y_ok, C * (m + 1))
                        for c in range(C):
                            last = nc.tensor.transpose(misc[:, c * 128:(c + 1) * 128], xn2[:, c, :], ident[:])
                        last.then_inc(xn2T_full, 1)
                    if u in (3, 5) and has(i, off):
                        weighted_values(u // 2 - 1)
                if has(i, off - 1):
                    m = n - 1
                    pe.wait_ge(xn2_lo_ok, m + 1)
                    for c in range(C):
                        cs = slice(c * 128, (c + 1) * 128)
                        last = exact(misc[:, c * E:(c + 1) * E], (xn2_hi[:, cs], xn2_lo[:, cs]), (rw_hi[:], rw_lo[:]))
                    last.then_inc(lg_full, 1)
                if has(i, off + 1):
                    m = n + 1
                    pe.wait_ge(s_used, U * (m + 1))
                    if has(i, off - 1):
                        pe.wait_ge(lg_ok, n)
                    elif has(i, off + 1):
                        pe.wait_ge(v_ok, m + 1)
                    for c in range(C):
                        last = nc.tensor.transpose(misc[0:H, c * 128:(c + 1) * 128], mx[:, c, :], ident[:])
                    last.then_inc(mT_full, 1)
                if has(i, off):
                    weighted_values(2)
                    weighted_values(3)

            over_batches(pe, first_half, second_half)


_INS = ['L0_attn_x', 'L0_attn_w_qkv', 'L0_attn_w_out', 'L0_attn_b_out', 'L0_ffn_router_w', 'L0_ffn_router_b',
        'L0_ffn_w1', 'L0_ffn_w3', 'L0_ffn_w2']
_OUTS = [((32, 256, 128), 'float32')]


def kernel(**inputs):
    import numpy as _np
    import concourse.bacc as _bacc
    from concourse import mybir as _mybir
    from concourse.bass_utils import run_bass_kernel_spmd as _run

    nc = _bacc.Bacc("TRN2", target_bir_lowering=False, num_devices=1)
    arrays, args = {}, []
    for name in _INS:
        a = _np.ascontiguousarray(inputs[name])
        arrays[f"in_{name}_dram"] = a
        args.append(nc.dram_tensor(f"in_{name}_dram", a.shape, _mybir.dt.from_np(a.dtype), kind="ExternalInput").ap())
    for i, (shape, dtype) in enumerate(_OUTS):
        dt = _mybir.dt.from_np(_np.dtype(dtype))
        args.append(nc.dram_tensor(f"out_{i}_dram", shape, dt, kind="ExternalOutput").ap())
    attention_then_experts_kernel(nc, *args)
    r = _run(nc, [arrays], core_ids=[0])
    got = tuple(r.results[0][f"out_{i}_dram"] for i in range(len(_OUTS)))
    return got[0]
```

```python
import concourse.bass as bass
from concourse import mybir
from contextlib import ExitStack


def attention_then_experts_kernel(nc: bass.Bass, x: bass.AP, w_qkv: bass.AP, w_out: bass.AP, b_out: bass.AP,
                                  router_w: bass.AP, router_b: bass.AP, w1: bass.AP, w3: bass.AP, w2: bass.AP,
                                  out: bass.AP):
    F32 = mybir.dt.float32
    F32R = mybir.dt.float32r
    ALU = mybir.AluOpType
    ACT = mybir.ActivationFunctionType
    AX = mybir.AxisListType

    B, S, D = x.shape
    E, _, F = w1.shape
    H = 16
    HD = D // H
    SCALE = float(HD) ** -0.5
    EPS = 1e-5
    C = S // 128
    G = H // 4
    FB = F // 128
    NB = E * FB
    U = G * C
    MROW = 96
    KROWS = MROW + 2
    UP = NB // 2

    scratch = nc.dram_tensor("qk_scratch", [4, 128, S], F32).ap()

    def row_to_all(ap, n):
        return bass.AP(ap.tensor, ap.offset, [[0, 128], [1, n]])

    ctx = ExitStack()
    with ctx:
        def sb(name, shape, dt=F32):
            return ctx.enter_context(nc.sbuf_tensor(name, shape, dt))

        def sem(name):
            return ctx.enter_context(nc.semaphore(name))

        ident = sb("ident", [128, 128])
        proj_T = sb("proj_T", [128, 4, D])
        w1_hi = sb("w1_hi", [128, E, F], F32R)
        w1_lo = sb("w1_lo", [128, E, F], F32R)
        w3_hi = sb("w3_hi", [128, E, F], F32R)
        w3_lo = sb("w3_lo", [128, E, F], F32R)
        w2_sb = sb("w2_sb", [128, NB, D])
        rw_raw = sb("rw_raw", [128, E])
        rw_hi = sb("rw_hi", [128, E], F32R)
        rw_lo = sb("rw_lo", [128, E], F32R)
        b_out_all = sb("b_out_all", [128, D])
        router_b_all = sb("router_b_all", [128, E])
        earlier = sb("earlier", [128, E, E])
        x_in = sb("x_in", [128, C, D])
        xn = sb("xn", [128, C, D])
        xn_T = sb("xn_T", [128, S])
        qk_split = sb("qk_split", [128, 4, S], F32R)
        q_stack = [sb(f"q_stack{i}", [128, H, S], F32R) for i in range(2)]
        k_stack = [sb(f"k_stack{i}", [128, H, S], F32R) for i in range(2)]
        v_pad = [sb(f"v_pad{i}", [128, C, H, 32]) for i in range(2)]
        mx = sb("mx", [128, C, H])
        m_split = sb("m_split", [H, 2, S], F32R)
        w_sq = sb("w_sq", [128, 2, 4 * S])
        poly = sb("poly", [128, U, 4 * S])
        o_T = sb("o_T", [128, G, S])
        den_r = sb("den_r", [128, C, H])
        attn = sb("attn", [128, C, D])
        attn_T = sb("attn_T", [128, S])
        x_res = sb("x_res", [128, C, D])
        x_resb = sb("x_resb", [128, C, D])
        y_acc = [sb(f"y_acc{i}", [128, C, D]) for i in range(2)]
        two = sb("two", [128, 1])
        stats = sb("stats", [128, 2 * C, 6])
        mean_var = sb("mean_var", [128, 2 * C, 2])
        eps_all = sb("eps_all", [128, 2 * C])
        minus_half = sb("minus_half", [128, 2 * C])
        three_halves = sb("three_halves", [128, 2 * C])
        half_var = sb("half_var", [128, 2 * C])
        var_eps = sb("var_eps", [128, 2 * C])
        ln_var = sb("ln_var", [128, 2 * C])
        rstd0 = sb("rstd0", [128, 2 * C])
        newton = sb("newton", [128, 2 * C])
        rstd = sb("rstd", [128, 2 * C])
        xn2 = sb("xn2", [128, C, D])
        xn2_hi = sb("xn2_hi", [128, S], F32R)
        xn2_lo = sb("xn2_lo", [128, S], F32R)
        silu_a = sb("silu_a", [128, 2, 2 * S])
        hid = sb("hid", [128, NB, S])
        logits = sb("logits", [128, C, E])
        top_l = sb("top_l", [128, C])
        shifted = sb("shifted", [128, C, E])
        exp_l = sb("exp_l", [128, C, E])
        above = sb("above", [128, C, E, E])
        equal = sb("equal", [128, C, E, E])
        rank = sb("rank", [128, C, E])
        chosen = sb("chosen", [128, C, E])
        chosen_sum = sb("chosen_sum", [128, C])
        chosen_r = sb("chosen_r", [128, C])
        gates = [sb(f"gates{i}", [128, C, E]) for i in range(2)]

        sc = ctx.enter_context(nc.psum_tensor("sc", [128, 2, 4 * S], F32))
        up_a = ctx.enter_context(nc.psum_tensor("up_a", [128, 2 * S], F32))
        up_b = ctx.enter_context(nc.psum_tensor("up_b", [128, 2 * S], F32))
        pv = ctx.enter_context(nc.psum_tensor("pv", [128, 2, S], F32))
        misc = ctx.enter_context(nc.psum_tensor("misc", [128, 512], F32))

        ld_w = sem("ld_w")
        ident_ok = sem("ident_ok")
        consts_ok = sem("consts_ok")
        consts_v = sem("consts_v")
        q_blank = sem("q_blank")
        k_blank = sem("k_blank")
        split_ok = sem("split_ok")
        wT_full = sem("wT_full")
        proj_ok = sem("proj_ok")
        x_loaded = sem("x_loaded")
        xr_loaded = sem("xr_loaded")
        xres_ok = sem("xres_ok")
        agg_ok = sem("agg_ok")
        var_ok = sem("var_ok")
        lnv_ok = sem("lnv_ok")
        rstd0_ok = sem("rstd0_ok")
        newton_step = sem("newton_step")
        rstd_ok = sem("rstd_ok")
        xn_ok = sem("xn_ok")
        xn2_ok = sem("xn2_ok")
        xnT_full = sem("xnT_full")
        xnT_ok = sem("xnT_ok")
        qk_full = sem("qk_full")
        qk_hi_ok = sem("qk_hi_ok")
        qk_ok = sem("qk_ok")
        v_full = sem("v_full")
        v_ok = sem("v_ok")
        qk_stored = sem("qk_stored")
        stacked = [sem(f"stacked{i}") for i in range(2)]
        s_full = sem("s_full")
        s_used = sem("s_used")
        mT_full = sem("mT_full")
        m_hi_ok = sem("m_hi_ok")
        m_ok = sem("m_ok")
        m_stacked = [sem(f"m_stacked{i}") for i in range(2)]
        w_full = sem("w_full")
        sq_ok = sem("sq_ok")
        poly_ok = sem("poly_ok")
        ln_ok = sem("ln_ok")
        p_ok = sem("p_ok")
        pv_full = sem("pv_full")
        o_ok0 = sem("o_ok0")
        o_ok1 = sem("o_ok1")
        oq_full = sem("oq_full")
        den_ok = sem("den_ok")
        attn_ok = sem("attn_ok")
        attnT_full = sem("attnT_full")
        attnT_ok = sem("attnT_ok")
        res_full = sem("res_full")
        y_ok = sem("y_ok")
        xn2T_full = sem("xn2T_full")
        xn2_hi_ok = sem("xn2_hi_ok")
        xn2_lo_ok = sem("xn2_lo_ok")
        lg_full = sem("lg_full")
        lg_ok = sem("lg_ok")
        shift_ok = sem("shift_ok")
        exp_ok = sem("exp_ok")
        route_step = sem("route_step")
        gates_ok = sem("gates_ok")
        a_full = sem("a_full")
        silu_ok = sem("silu_ok")
        b_full = sem("b_full")
        hid_ok = sem("hid_ok")
        down_full = sem("down_full")
        acc_ok = sem("acc_ok")
        stored = [sem(f"stored{i}") for i in range(2)]

        ROUTE = 6

        def no(i, off):
            return 2 * i + off

        def has(i, off):
            return not isinstance(i, int) or 0 <= no(i, off) < B

        def after(eng, s, count):
            if not isinstance(count, int) or count > 0:
                eng.wait_ge(s, count)

        def pair_count(i, off, each):
            return (i + off // 2 + 1) * each

        def over_batches(eng, half_a, half_b):
            for n in range(-2, 2):
                half_a(n // 2, n % 2)
                half_b(n // 2, n % 2)
            with eng.Fori(1, B // 2 - 1) as i:
                for off in range(2):
                    half_a(i, off)
                    half_b(i, off)
            for n in range(B - 2, B + 2):
                half_a(n // 2, n % 2)
                half_b(n // 2, n % 2)

        block = ctx.enter_context(nc.Block())

        @block.sync
        def _(sp):
            sp.dma_start(poly[:, 4, 0:3 * D].rearrange("p (s d) -> p s d", s=3),
                         w_qkv.rearrange("(s o) d -> o s d", s=3)).then_inc(ld_w, 16)
            sp.dma_start(poly[:, 4, 3 * D:4 * D], w_out).then_inc(ld_w, 16)
            sp.dma_start(b_out_all[:], row_to_all(b_out, D)).then_inc(ld_w, 16)
            sp.dma_start(router_b_all[:], row_to_all(router_b, E)).then_inc(ld_w, 16)
            sp.dma_start(rw_raw[:], router_w).then_inc(ld_w, 16)
            sp.dma_start(poly[:, 0:2, :].rearrange("p a (b f) -> p (a b) f", b=2),
                         w1.rearrange("e d f -> d e f")).then_inc(ld_w, 16)
            sp.dma_start(poly[:, 2:4, :].rearrange("p a (b f) -> p (a b) f", b=2),
                         w3.rearrange("e d f -> d e f")).then_inc(ld_w, 16)
            sp.dma_start(w2_sb[:], w2.rearrange("e (c p) d -> p (e c) d", p=128)).then_inc(ld_w, 16)

            def value(v):
                if not isinstance(v, int):
                    sp.compute_val(v)
                return v

            def address(offset):
                value(offset)
                value(offset * 4)
                return offset

            def batch_at(t, offset):
                return bass.AP(t.tensor, offset, [[D, 128], [128 * D, C], [1, D]])

            def first_half(i, off):
                n = no(i, off)
                par = (off + 1) % 2
                xn_used, x_from, y_from = value(n + 2), address((n + 2) * S * D), address(n * S * D)
                split, scratch_read, w_used = value(n + 2), value(pair_count(i, off, 128)), value(U * n)
                stored_qk, res_used = value(16 * (n + 2)), value(n)
                if has(i, off + 2):
                    after(sp, xn_ok, xn_used)
                    sp.dma_start(x_in[:], batch_at(x, x_from)).then_inc(x_loaded, 16)
                if has(i, off + 1):
                    after(sp, qk_ok, split)
                    after(sp, stacked[1 - par], scratch_read)
                    sp.dma_start(scratch.rearrange("a p t -> p a t"), qk_split[:].bitcast(F32)).then_inc(qk_stored, 16)
                    after(sp, w_full, w_used)
                    sp.wait_ge(qk_stored, stored_qk)
                    if isinstance(i, int) and 0 <= n + 1 < 2:
                        sp.wait_ge(q_blank, n + 2)
                        sp.wait_ge(k_blank, 2 * (n + 2))
                    for stack, parts in ((q_stack, (0, 0, 1, 1)), (k_stack, (2, 3, 2, 3))):
                        for r, part in enumerate(parts):
                            sp.dma_start(stack[par][HD * r:HD * (r + 1), :, :].bitcast(F32),
                                         scratch[part].rearrange("(h d) t -> d h t", d=HD)).then_inc(stacked[par], 16)
                if has(i, off):
                    after(sp, xres_ok, res_used)
                    sp.dma_start(x_res[:], batch_at(x, y_from)).then_inc(xr_loaded, 16)

            def second_half(i, off):
                n = no(i, off)
                m_split_at, added, out_at = value(n + 2), value(E * C * (n - 1)), address((n - 2) * S * D)
                if has(i, off + 1):
                    par = (off + 1) % 2
                    sp.wait_ge(m_ok, m_split_at)
                    for a in range(2):
                        sp.dma_start(q_stack[par][MROW + a:MROW + a + 1, :, :].bitcast(F32),
                                     m_split[:, a, :].bitcast(F32)).then_inc(m_stacked[par], 16)
                if has(i, off - 2):
                    par = off % 2
                    sp.wait_ge(acc_ok, added)
                    sp.dma_start(batch_at(out, out_at), y_acc[par][:]).then_inc(stored[par], 16)

            over_batches(sp, first_half, second_half)
            for par in range(2):
                sp.wait_ge(stored[par], 16 * (B // 2))

        @block.gpsimd
        def _(pool):
            nc.gpsimd.memset(ident[:], 0.0).then_inc(consts_ok, 1)
            nc.gpsimd.memset(earlier[:], 1.0).then_inc(consts_ok, 1)
            nc.gpsimd.memset(eps_all[:], EPS)
            nc.gpsimd.memset(minus_half[:], -0.5)
            nc.gpsimd.memset(three_halves[:], 1.5).then_inc(consts_ok, 1)
            pool.wait_ge(consts_ok, 3)
            nc.gpsimd.affine_select(out=ident[:], in_=ident[:], compare_op=ALU.not_equal, fill=1.0, base=0,
                                    pattern=[[-1, 128]], channel_multiplier=1).then_inc(ident_ok, 1)
            nc.gpsimd.affine_select(out=earlier[:], in_=earlier[:], compare_op=ALU.is_ge, fill=0.0, base=-1,
                                    pattern=[[1, E], [-1, E]], channel_multiplier=0).then_inc(consts_ok, 1)
            pool.wait_ge(consts_ok, 4)
            for par in range(2):
                nc.gpsimd.memset(k_stack[par][0:MROW].bitcast(F32), 0.0).then_inc(k_blank, 1)
                pool.wait_ge(k_blank, 2 * par + 1)
                nc.gpsimd.memset(k_stack[par][MROW:KROWS].bitcast(F32), 1.0).then_inc(k_blank, 1)
                pool.wait_ge(k_blank, 2 * par + 2)
            pool.wait_ge(ld_w, 16 * 8)

            def first_half(i, off):
                if has(i, off):
                    m = no(i, off)
                    pool.wait_ge(xr_loaded, 16 * (m + 1))
                    after(pool, y_ok, C * m)
                    for c in range(C):
                        last = nc.gpsimd.tensor_tensor(x_resb[:, c, :], x_res[:, c, :], b_out_all[:], ALU.add)
                    last.then_inc(xres_ok, 1)

            def second_half(i, off):
                lo, hi = (0 if has(i, off - 1) else C), (2 * C if has(i, off + 2) else C)
                if lo < hi:
                    n = no(i, off)
                    k = n + 2
                    s = slice(lo, hi)
                    pool.wait_ge(agg_ok, k + 1)
                    nc.gpsimd.tensor_tensor(var_eps[:, s], mean_var[:, s, 1], eps_all[:, s], ALU.add).then_inc(var_ok, 1)
                    pool.wait_ge(var_ok, k + 1)
                    nc.gpsimd.tensor_tensor(half_var[:, s], var_eps[:, s], minus_half[:, s],
                                            ALU.mult).then_inc(newton_step, 1)
                    pool.wait_ge(rstd0_ok, k + 1)
                    nc.gpsimd.tensor_tensor(newton[:, s], rstd0[:, s], rstd0[:, s], ALU.mult).then_inc(newton_step, 1)
                    pool.wait_ge(newton_step, 4 * k + 2)
                    nc.gpsimd.tensor_tensor(newton[:, s], newton[:, s], half_var[:, s], ALU.mult).then_inc(newton_step, 1)
                    pool.wait_ge(newton_step, 4 * k + 3)
                    nc.gpsimd.tensor_tensor(newton[:, s], newton[:, s], three_halves[:, s],
                                            ALU.add).then_inc(newton_step, 1)
                    pool.wait_ge(newton_step, 4 * k + 4)
                    if has(i, off - 1):
                        after(pool, xn2T_full, n - 1)
                    if has(i, off + 2):
                        after(pool, xnT_full, n + 2)
                    nc.gpsimd.tensor_tensor(rstd[:, s], rstd0[:, s], newton[:, s], ALU.mult).then_inc(rstd_ok, 1)
                    nc.gpsimd.drain()
                    for t in range(lo, hi):
                        dst, src = ((xn2[:, t, :], y_acc[(off - 1) % 2][:, t, :]) if t < C
                                    else (xn[:, t - C, :], x_in[:, t - C, :]))
                        ins = nc.gpsimd.tensor_scalar(dst, src, mean_var[:, t, 0:1], rstd[:, t:t + 1], ALU.subtract,
                                                      ALU.mult)
                        if t == C - 1:
                            ins.then_inc(xn2_ok, 1)
                        if t == 2 * C - 1:
                            ins.then_inc(xn_ok, 1)

            over_batches(pool, first_half, second_half)

        @block.scalar
        def _(act):
            def first_half(i, off):
                n = no(i, off)
                act.preload_act_table_set("silu_and_others")
                if has(i, off + 1):
                    m = n + 1
                    act.wait_ge(xnT_full, m + 1)
                    after(act, v_full, m)
                    nc.scalar.copy(xn_T[:], misc[:, 0:S]).then_inc(xnT_ok, 1)
                for u in range(U + 1):
                    if u < U and has(i, off - 2):
                        k = UP * (n - 2) + u
                        act.wait_ge(a_full, k + 1)
                        after(act, hid_ok, k - 1 if u > 1 else k - u)
                        nc.scalar.activation(silu_a[:, u % 2, :], up_a[:], ACT.Silu).then_inc(silu_ok, 1)
                    if u == 2 and has(i, off + 1):
                        m, par = n + 1, (off + 1) % 2
                        act.wait_ge(v_full, m + 1)
                        act.wait_ge(consts_v, 4)
                        after(act, pv_full, G * (m - 1))
                        for c in range(C):
                            last = nc.scalar.copy(v_pad[par][:, c, :, 0:HD],
                                                  misc[:, c * D:(c + 1) * D].rearrange("p (h d) -> p h d", d=HD))
                        last.then_inc(v_ok, 1)
                    if u == 5 and has(i, off - 1):
                        m = n - 1
                        act.wait_ge(attnT_full, m + 1)
                        after(act, res_full, m)
                        nc.scalar.copy(attn_T[:], misc[:, 0:S]).then_inc(attnT_ok, 1)
                    if u > 0 and has(i, off):
                        v = u - 1
                        k = U * n + v
                        act.wait_ge(w_full, k + 1)
                        after(act, poly_ok, k - 1 if v > 1 else k - v)
                        nc.scalar.activation(w_sq[:, v % 2, :], sc[:, v % 2, :], ACT.Square).then_inc(sq_ok, 1)
                    if u == 0 and has(i, off - 1):
                        act.wait_ge(pv_full, G * n)
                        after(act, oq_full, C * (n - 1))
                        nc.scalar.copy(o_T[:, 2:4, :], pv[:]).then_inc(o_ok1, 1)
                    if u == 0 and has(i, off + 1):
                        m = n + 1
                        act.wait_ge(qk_full, m + 1)
                        after(act, qk_stored, 16 * m)
                        nc.scalar.copy(qk_split[:, 0, :], misc[:, 0:S])
                        nc.scalar.mul(qk_split[:, 2, :], misc[:, S:2 * S], -SCALE).then_inc(qk_hi_ok, 1)

            def second_half(i, off):
                n = no(i, off)
                act.preload_act_table_set("natural_log_exp_and_others")

                def log_of(g):
                    act.wait_ge(poly_ok, U * n + C * (g + 1))
                    nc.scalar.activation(poly[:, C * g:C * (g + 1), :], poly[:, C * g:C * (g + 1), :], ACT.Ln,
                                         bias=two[:]).then_inc(ln_ok, 1)

                def weights_of(g):
                    act.wait_ge(ln_ok, G * n + g + 1)
                    nc.scalar.activation(poly[:, C * g:C * (g + 1), :], poly[:, C * g:C * (g + 1), :], ACT.Exp,
                                         scale=-1.0).then_inc(p_ok, 1)

                if has(i, off):
                    log_of(0)
                lo, hi = (0 if has(i, off - 1) else C), (2 * C if has(i, off + 2) else C)
                if lo < hi:
                    k = n + 2
                    s = slice(lo, hi)
                    act.wait_ge(var_ok, k + 1)
                    nc.scalar.activation(ln_var[:, s], var_eps[:, s], ACT.Ln).then_inc(lnv_ok, 1)
                    act.wait_ge(lnv_ok, k + 1)
                    after(act, rstd_ok, k)
                    nc.scalar.activation(rstd0[:, s], ln_var[:, s], ACT.Exp, scale=-0.5).then_inc(rstd0_ok, 1)
                if has(i, off):
                    log_of(1)
                for g in range(G):
                    if has(i, off):
                        if 0 < g < G - 1:
                            log_of(g + 1)
                        weights_of(g)
                    if g == 1 and has(i, off - 1):
                        m = n - 1
                        act.wait_ge(xn2T_full, m + 1)
                        after(act, b_full, UP * m)
                        after(act, lg_full, m)
                        nc.scalar.copy(xn2_hi[:], misc[:, 0:S]).then_inc(xn2_hi_ok, 1)
                if has(i, off - 1):
                    m = n - 1
                    act.wait_ge(shift_ok, m + 1)
                    nc.scalar.activation(exp_l[:], shifted[:], ACT.Exp).then_inc(exp_ok, 1)

            act.wait_ge(consts_v, 4)
            over_batches(act, first_half, second_half)

        @block.vector
        def _(dve):
            nc.vector.memset(two[:], 2.0).then_inc(consts_v, 1)
            for par in range(2):
                nc.vector.memset(q_stack[par][0:MROW].bitcast(F32), 0.0).then_inc(q_blank, 1)
            for par in range(2):
                nc.vector.memset(v_pad[par][:], 0.0)
            nc.vector.memset(gates[0][:], 0.0).then_inc(consts_v, 1)
            dve.wait_ge(consts_v, 2)
            for par in range(2):
                nc.vector.memset(v_pad[par][:, :, :, HD], 1.0).then_inc(consts_v, 1)
            dve.wait_ge(wT_full, 1)
            nc.vector.tensor_copy(proj_T[:].rearrange("p s d -> p (s d)"), misc[:]).then_inc(proj_ok, 1)
            dve.wait_ge(ld_w, 16 * 8)
            raw1 = poly[:, 0:2, :].rearrange("p a n -> p (a n)")
            raw3 = poly[:, 2:4, :].rearrange("p a n -> p (a n)")
            splits = ((w1_hi[:].rearrange("p e f -> p (e f)"), w1_lo[:].rearrange("p e f -> p (e f)"), raw1),
                      (w3_hi[:].rearrange("p e f -> p (e f)"), w3_lo[:].rearrange("p e f -> p (e f)"), raw3),
                      (rw_hi[:], rw_lo[:], rw_raw[:]))
            for k, (hi, lo, raw) in enumerate(splits):
                nc.vector.tensor_copy(hi, raw).then_inc(split_ok, 1)
                dve.wait_ge(split_ok, 2 * k + 1)
                nc.vector.tensor_tensor(lo, raw, hi.bitcast(F32), ALU.subtract).then_inc(split_ok, 1)

            def first_half(i, off):
                n = no(i, off)
                for u in range(U + 1):
                    if u < U and has(i, off - 2):
                        k = UP * (n - 2) + u
                        dve.wait_ge(b_full, k + 1)
                        dve.wait_ge(silu_ok, k + 1)
                        if u == 0:
                            after(dve, down_full, E * (n - 2))
                        nc.vector.tensor_tensor(hid[:, 2 * u:2 * u + 2, :].rearrange("p a t -> p (a t)"),
                                                silu_a[:, u % 2, :], up_b[:], ALU.mult).then_inc(hid_ok, 1)
                    if u > 0 and has(i, off):
                        v = u - 1
                        k = U * n + v
                        dve.wait_ge(sq_ok, k + 1)
                        if v % C == 0:
                            after(dve, pv_full, G * (n - 1) + v // C + 1)
                        nc.vector.scalar_tensor_tensor(poly[:, v, :], w_sq[:, v % 2, :], 3.0, sc[:, v % 2, :],
                                                       ALU.add, ALU.mult).then_inc(poly_ok, 1)
                    if u == 0 and has(i, off + 1):
                        m = n + 1
                        dve.wait_ge(qk_hi_ok, m + 1)
                        nc.vector.tensor_tensor(qk_split[:, 1, :], misc[:, 0:S], qk_split[:, 0, :].bitcast(F32),
                                                ALU.subtract)
                        nc.vector.scalar_tensor_tensor(qk_split[:, 3, :], misc[:, S:2 * S], -SCALE,
                                                       qk_split[:, 2, :].bitcast(F32), ALU.mult,
                                                       ALU.subtract).then_inc(qk_ok, 1)
                    if u == 1 and has(i, off + 2):
                        dve.wait_ge(x_loaded, 16 * (n + 3))
                        for c in range(C):
                            nc.vector.bn_stats(stats[:, C + c, :], x_in[:, c, :])
                    if u in (2, 3) and has(i, off - 1):
                        m, c = n - 1, u - 2
                        by_head = misc[:].rearrange("p (h e) -> p h e", e=32)
                        dve.wait_ge(oq_full, C * m + c + 1)
                        nc.vector.reciprocal(den_r[:, c, :], by_head[:, :, HD]).then_inc(den_ok, 1)
                        dve.wait_ge(den_ok, C * m + c + 1)
                        after(dve, attnT_full, m)
                        nc.vector.tensor_tensor(attn[:, c, :].rearrange("p (h d) -> p h d", d=HD),
                                                by_head[:, :, 0:HD],
                                                den_r[:, c, :].unsqueeze(2).to_broadcast([128, H, HD]),
                                                ALU.mult).then_inc(attn_ok, 1)
                    if u == 6 and has(i, off - 1):
                        m, par = n - 1, (off - 1) % 2
                        dve.wait_ge(res_full, m + 1)
                        dve.wait_ge(xres_ok, m + 1)
                        after(dve, stored[par], pair_count(i, off - 3, 16))
                        for c in range(C):
                            nc.vector.tensor_tensor(y_acc[par][:, c, :], misc[:, c * D:(c + 1) * D],
                                                    x_resb[:, c, :], ALU.add).then_inc(y_ok, 1)

            def second_half(i, off):
                n = no(i, off)
                lo, hi = (0 if has(i, off - 1) else C), (2 * C if has(i, off + 2) else C)
                k = n + 2
                if lo < hi:
                    if has(i, off - 1):
                        dve.wait_ge(y_ok, C * n)
                    after(dve, xn_ok, min(n + 2, B) if isinstance(i, int) else n + 2)
                    after(dve, xn2_ok, n - 1)
                    for c in range(C if has(i, off - 1) else 0):
                        nc.vector.bn_stats(stats[:, c, :], y_acc[(off - 1) % 2][:, c, :])
                    nc.vector.drain()
                    for s in range(lo, hi):
                        last = nc.vector.bn_aggr(mean_var[:, s, :], stats[:, s, :])
                    last.then_inc(agg_ok, 1)

                def scores_max(u):
                    g, c = u // C, u % C
                    dve.wait_ge(s_full, U * (n + 1) + u + 1)
                    if u == 0:
                        after(dve, mT_full, n + 1)
                    nc.vector.tensor_reduce(mx[:, c, 4 * g:4 * g + 4],
                                            sc[:, u % 2, :].rearrange("p (j t) -> p j t", j=4), AX.X, ALU.min,
                                            negate=True).then_inc(s_used, 1)

                def add_expert(e):
                    m, par = n - 2, off % 2
                    dve.wait_ge(down_full, E * m + e + 1)
                    bank = (up_a, up_b)[e % 2]
                    for c in range(C):
                        after(dve, acc_ok, E * C * m + C * e - (C - 1) + c if e else 0)
                        nc.vector.scalar_tensor_tensor(y_acc[par][:, c, :], bank[:, c * D:(c + 1) * D],
                                                       gates[par][:, c, e:e + 1], y_acc[par][:, c, :], ALU.mult,
                                                       ALU.add).then_inc(acc_ok, 1)

                def route_logits():
                    m = n - 1
                    dve.wait_ge(lg_full, m + 1)
                    for c in range(C):
                        last = nc.vector.tensor_tensor(logits[:, c, :], misc[:, c * E:(c + 1) * E], router_b_all[:],
                                                       ALU.add)
                    last.then_inc(lg_ok, 1)
                    dve.wait_ge(lg_ok, m + 1)
                    nc.vector.tensor_reduce(top_l[:], logits[:], AX.X, ALU.max).then_inc(route_step, 1)
                    dve.wait_ge(route_step, ROUTE * m + 1)
                    after(dve, exp_ok, m)
                    nc.vector.tensor_tensor(shifted[:], logits[:], top_l[:].unsqueeze(2).to_broadcast([128, C, E]),
                                            ALU.subtract).then_inc(shift_ok, 1)

                def route_ranks():
                    m = n - 1
                    for c in range(C):
                        l_j = logits[:, c, :].unsqueeze(1).to_broadcast([128, E, E])
                        l_i = logits[:, c, :].unsqueeze(2).to_broadcast([128, E, E])
                        nc.vector.tensor_tensor(above[:, c], l_j, l_i, ALU.is_gt)
                        last = nc.vector.tensor_tensor(equal[:, c], l_j, l_i, ALU.is_equal)
                    last.then_inc(route_step, 1)
                    dve.wait_ge(route_step, ROUTE * m + 2)
                    for c in range(C):
                        last = nc.vector.tensor_tensor(equal[:, c], equal[:, c], earlier[:], ALU.mult)
                    last.then_inc(route_step, 1)
                    dve.wait_ge(route_step, ROUTE * m + 3)
                    nc.vector.tensor_tensor(above[:].rearrange("p c i j -> p (c i j)"),
                                            above[:].rearrange("p c i j -> p (c i j)"),
                                            equal[:].rearrange("p c i j -> p (c i j)"), ALU.add).then_inc(route_step, 1)
                    dve.wait_ge(route_step, ROUTE * m + 4)
                    nc.vector.tensor_reduce(rank[:], above[:], AX.X, ALU.add).then_inc(route_step, 1)

                def route_gates():
                    m, par = n - 1, (off - 1) % 2
                    dve.wait_ge(route_step, ROUTE * m + 5)
                    dve.wait_ge(exp_ok, m + 1)
                    nc.vector.scalar_tensor_tensor(chosen[:], rank[:], 1.5, exp_l[:], ALU.is_lt,
                                                   ALU.mult).then_inc(gates_ok, 1)
                    dve.wait_ge(gates_ok, 3 * m + 1)
                    nc.vector.tensor_reduce(chosen_sum[:], chosen[:], AX.X, ALU.add).then_inc(gates_ok, 1)
                    dve.wait_ge(gates_ok, 3 * m + 2)
                    nc.vector.reciprocal(chosen_r[:], chosen_sum[:]).then_inc(gates_ok, 1)
                    dve.wait_ge(gates_ok, 3 * m + 3)
                    nc.vector.tensor_tensor(gates[par][:], chosen[:],
                                            chosen_r[:].unsqueeze(2).to_broadcast([128, C, E]),
                                            ALU.mult).then_inc(route_step, 1)

                for u in range(U):
                    if has(i, off + 1):
                        scores_max(u)
                    if u in (1, 2) and has(i, off - 2):
                        if u == 1:
                            after(dve, route_step, ROUTE * (n - 1))
                        add_expert(u - 1)
                    if u == 5 and has(i, off - 1):
                        m = n - 1
                        dve.wait_ge(xn2_hi_ok, m + 1)
                        nc.vector.tensor_tensor(xn2_lo[:], misc[:, 0:S], xn2_hi[:].bitcast(F32),
                                                ALU.subtract).then_inc(xn2_lo_ok, 1)
                    if u == 6 and has(i, off):
                        dve.wait_ge(pv_full, G * n + 2)
                        after(dve, oq_full, C * n)
                        nc.vector.tensor_copy(o_T[:, 0:2, :], pv[:]).then_inc(o_ok0, 1)
                if has(i, off - 1):
                    route_logits()
                if has(i, off - 2):
                    add_expert(2)
                if has(i, off + 1):
                    m = n + 1
                    dve.wait_ge(mT_full, m + 1)
                    after(dve, m_stacked[off % 2], pair_count(i, off, 32))
                    nc.vector.tensor_scalar(m_split[:, 0, :], misc[0:H, 0:S], 1.0, None, ALU.add).then_inc(m_hi_ok, 1)
                    dve.wait_ge(m_hi_ok, m + 1)
                    nc.vector.scalar_tensor_tensor(m_split[:, 1, :], misc[0:H, 0:S], 1.0,
                                                   m_split[:, 0, :].bitcast(F32), ALU.add,
                                                   ALU.subtract).then_inc(m_ok, 1)
                if has(i, off - 2):
                    add_expert(3)
                if has(i, off - 1):
                    route_ranks()
                    route_gates()

            dve.wait_ge(consts_ok, 4)
            over_batches(dve, first_half, second_half)

        @block.tensor
        def _(pe):
            pe.wait_ge(ident_ok, 1)
            pe.wait_ge(ld_w, 16 * 8)
            for s in range(4):
                last = nc.tensor.transpose(misc[:, s * D:(s + 1) * D], poly[:, 4, s * D:(s + 1) * D], ident[:])
            last.then_inc(wT_full, 1)
            pe.wait_ge(proj_ok, 1)
            pe.wait_ge(split_ok, 6)
            pe.wait_ge(k_blank, 4)
            pe.wait_ge(q_blank, 2)

            def exact(dst, lhs, rhs):
                terms = ((0, 0), (0, 1), (1, 0))
                for k, (a, b) in enumerate(terms):
                    last = nc.tensor.matmul(dst, lhs[a], rhs[b], start=(k == 0), stop=(k == len(terms) - 1))
                return last

            def weighted_values(i, off, g):
                n, par = no(i, off), off % 2
                pe.wait_ge(p_ok, G * n + g + 1)
                if g == 0:
                    pe.wait_ge(v_ok, n + 1)
                    after(pe, o_ok1, n)
                if g == 2:
                    pe.wait_ge(o_ok0, n + 1)
                for c in range(C):
                    for j in range(4):
                        last = nc.tensor.matmul(pv[32 * j:32 * j + 32, g % 2, :], v_pad[par][:, c, 4 * g + j, :],
                                                poly[:, C * g + c, j * S:(j + 1) * S], start=(c == 0),
                                                stop=(c == C - 1))
                last.then_inc(pv_full, 1)

            def first_half(i, off):
                n = no(i, off)

                def up(u, dst, hi, lo, full):
                    for half in range(2):
                        e, f = divmod(2 * u + half, FB)
                        fs = slice(f * 128, (f + 1) * 128)
                        last = exact(dst[:, half * S:(half + 1) * S], (hi[:, e, fs], lo[:, e, fs]),
                                     (xn2_hi[:], xn2_lo[:]))
                    last.then_inc(full, 1)

                def distances(u):
                    par = off % 2
                    g, c = u // C, u % C
                    if u < 2:
                        pe.wait_ge(s_used, U * (n + 1) - 1 + u)
                    else:
                        pe.wait_ge(poly_ok, U * n + u - 1)
                    if u == 0:
                        pe.wait_ge(m_stacked[par], pair_count(i, off, 32))
                    for j in range(4):
                        last = nc.tensor.matmul(sc[:, u % 2, j * S:(j + 1) * S],
                                                k_stack[par][0:KROWS, 4 * g + j, c * 128:(c + 1) * 128],
                                                q_stack[par][0:KROWS, 4 * g + j, :], start=True, stop=True)
                    last.then_inc(w_full, 1)

                for u in range(U + 1):
                    if u < U and has(i, off - 2):
                        m = n - 2
                        after(pe, silu_ok, UP * m + u)
                        if u == 0:
                            after(pe, acc_ok, E * C * m)
                            pe.wait_ge(xn2_lo_ok, m + 1)
                        up(u, up_a, w1_hi, w1_lo, a_full)
                    if u > 0 and has(i, off):
                        distances(u - 1)
                    if u < U and has(i, off - 2):
                        after(pe, hid_ok, UP * (n - 2) + u)
                        up(u, up_b, w3_hi, w3_lo, b_full)
                    if u == 0 and has(i, off - 1):
                        weighted_values(i, off - 1, 3)
                    if u == 0 and has(i, off + 1):
                        m = n + 1
                        pe.wait_ge(xnT_ok, m + 1)
                        nc.tensor.matmul(misc[:, 0:S], proj_T[:, 0, :], xn_T[:], start=True, stop=True)
                        nc.tensor.matmul(misc[:, S:2 * S], proj_T[:, 1, :], xn_T[:], start=True,
                                         stop=True).then_inc(qk_full, 1)
                    if u == 1 and has(i, off + 1):
                        m = n + 1
                        pe.wait_ge(qk_ok, m + 1)
                        for c in range(C):
                            last = nc.tensor.matmul(misc[:, c * D:(c + 1) * D], xn_T[:, c * 128:(c + 1) * 128],
                                                    proj_T[:, 2, :], start=True, stop=True)
                        last.then_inc(v_full, 1)
                    if u in (2, 3) and has(i, off - 1):
                        m, c = n - 1, u - 2
                        if c == 0:
                            pe.wait_ge(o_ok1, m + 1)
                            pe.wait_ge(o_ok0, m + 1)
                            if has(i, off + 1):
                                pe.wait_ge(v_ok, n + 2)
                            else:
                                pe.wait_ge(lg_ok, m)
                        else:
                            pe.wait_ge(attn_ok, C * m + c)
                        for g in range(G):
                            last = nc.tensor.transpose(misc[:, g * 128:(g + 1) * 128],
                                                       o_T[:, g, c * 128:(c + 1) * 128], ident[:])
                        last.then_inc(oq_full, 1)
                    if u == 4 and has(i, off - 1):
                        m = n - 1
                        pe.wait_ge(attn_ok, C * (m + 1))
                        for c in range(C):
                            last = nc.tensor.transpose(misc[:, c * 128:(c + 1) * 128], attn[:, c, :], ident[:])
                        last.then_inc(attnT_full, 1)
                    if u == 5 and has(i, off - 1):
                        m = n - 1
                        pe.wait_ge(attnT_ok, m + 1)
                        for c in range(C):
                            last = nc.tensor.matmul(misc[:, c * D:(c + 1) * D], attn_T[:, c * 128:(c + 1) * 128],
                                                    proj_T[:, 3, :], start=True, stop=True)
                        last.then_inc(res_full, 1)

            def second_half(i, off):
                n = no(i, off)

                def scores(u):
                    m, par = n + 1, (off + 1) % 2
                    g, c = u // C, u % C
                    if u < 2:
                        after(pe, poly_ok, U * m - 1 + u)
                        if u == 0:
                            pe.wait_ge(stacked[par], pair_count(i, off + 1, 128))
                    else:
                        pe.wait_ge(s_used, U * m + u - 1)
                    for j in range(4):
                        last = nc.tensor.matmul(sc[:, u % 2, j * S:(j + 1) * S],
                                                q_stack[par][0:MROW, 4 * g + j, c * 128:(c + 1) * 128],
                                                k_stack[par][0:MROW, 4 * g + j, :], start=True, stop=True)
                    last.then_inc(s_full, 1)

                def down(e):
                    m = n - 2
                    bank = (up_a, up_b)[e % 2]
                    if e == 0:
                        pe.wait_ge(hid_ok, UP * (m + 1))
                    if e >= 2:
                        pe.wait_ge(acc_ok, E * C * m + C * (e - 1))
                    for c in range(C):
                        for f in range(FB):
                            last = nc.tensor.matmul(bank[:, c * D:(c + 1) * D], hid[:, FB * e + f, c * 128:(c + 1) * 128],
                                                    w2_sb[:, FB * e + f, :], start=(f == 0), stop=(f == FB - 1))
                    last.then_inc(down_full, 1)

                def maxima_T():
                    pe.wait_ge(s_used, U * (n + 2))
                    if has(i, off - 1):
                        pe.wait_ge(lg_ok, n)
                    else:
                        pe.wait_ge(v_ok, n + 2)
                    for c in range(C):
                        last = nc.tensor.transpose(misc[0:H, c * 128:(c + 1) * 128], mx[:, c, :], ident[:])
                    last.then_inc(mT_full, 1)

                def router_operand():
                    m = n - 1
                    pe.wait_ge(xn2_ok, m + 1)
                    pe.wait_ge(y_ok, C * (m + 1))
                    for c in range(C):
                        last = nc.tensor.transpose(misc[:, c * 128:(c + 1) * 128], xn2[:, c, :], ident[:])
                    last.then_inc(xn2T_full, 1)

                def router_logits():
                    m = n - 1
                    pe.wait_ge(xn2_lo_ok, m + 1)
                    for c in range(C):
                        cs = slice(c * 128, (c + 1) * 128)
                        last = exact(misc[:, c * E:(c + 1) * E], (xn2_hi[:, cs], xn2_lo[:, cs]), (rw_hi[:], rw_lo[:]))
                    last.then_inc(lg_full, 1)

                if has(i, off - 2):
                    down(0)
                for u in range(U):
                    if has(i, off + 1):
                        scores(u)
                    if u == 1 and has(i, off - 2):
                        down(1)
                    if u in (4, 6) and has(i, off):
                        weighted_values(i, off, u // 2 - 2)
                    if u == 4 and has(i, off - 1):
                        router_operand()
                    if u == 5 and has(i, off - 2):
                        down(2)
                    if u == 7 and has(i, off - 1):
                        router_logits()
                if has(i, off - 2):
                    down(3)
                if has(i, off + 1):
                    maxima_T()
                if has(i, off):
                    weighted_values(i, off, 2)
                if has(i, off + 2):
                    m = n + 2
                    pe.wait_ge(xn_ok, m + 1)
                    after(pe, m_ok, m)
                    for c in range(C):
                        last = nc.tensor.transpose(misc[:, c * 128:(c + 1) * 128], xn[:, c, :], ident[:])
                    last.then_inc(xnT_full, 1)

            over_batches(pe, first_half, second_half)


_INS = ['L0_attn_x', 'L0_attn_w_qkv', 'L0_attn_w_out', 'L0_attn_b_out', 'L0_ffn_router_w', 'L0_ffn_router_b',
        'L0_ffn_w1', 'L0_ffn_w3', 'L0_ffn_w2']
_OUTS = [((32, 256, 128), 'float32')]


def kernel(**inputs):
    import numpy as _np
    import concourse.bacc as _bacc
    from concourse import mybir as _mybir
    from concourse.bass_utils import run_bass_kernel_spmd as _run

    nc = _bacc.Bacc("TRN2", target_bir_lowering=False, num_devices=1)
    arrays, args = {}, []
    for name in _INS:
        a = _np.ascontiguousarray(inputs[name])
        arrays[f"in_{name}_dram"] = a
        args.append(nc.dram_tensor(f"in_{name}_dram", a.shape, _mybir.dt.from_np(a.dtype), kind="ExternalInput").ap())
    for i, (shape, dtype) in enumerate(_OUTS):
        dt = _mybir.dt.from_np(_np.dtype(dtype))
        args.append(nc.dram_tensor(f"out_{i}_dram", shape, dt, kind="ExternalOutput").ap())
    attention_then_experts_kernel(nc, *args)
    r = _run(nc, [arrays], core_ids=[0])
    got = tuple(r.results[0][f"out_{i}_dram"] for i in range(len(_OUTS)))
    return got[0]
```

```python
import concourse.bass as bass
from concourse import mybir
from contextlib import ExitStack


def attention_then_experts_kernel(nc: bass.Bass, x: bass.AP, w_qkv: bass.AP, w_out: bass.AP, b_out: bass.AP,
                                  router_w: bass.AP, router_b: bass.AP, w1: bass.AP, w3: bass.AP, w2: bass.AP,
                                  out: bass.AP):
    F32 = mybir.dt.float32
    F32R = mybir.dt.float32r
    ALU = mybir.AluOpType
    ACT = mybir.ActivationFunctionType
    AX = mybir.AxisListType

    B, S, D = x.shape
    E, _, F = w1.shape
    H = 16
    HD = D // H
    SCALE = float(HD) ** -0.5
    EPS = 1e-5
    C = S // 128
    G = H // 4
    FB = F // 128
    NB = E * FB
    U = G * C
    MROW = 96
    KROWS = MROW + 2
    UP = NB // 2

    scratch = nc.dram_tensor("qk_scratch", [4, 128, S], F32).ap()

    def row_to_all(ap, n):
        return bass.AP(ap.tensor, ap.offset, [[0, 128], [1, n]])

    ctx = ExitStack()
    with ctx:
        def sb(name, shape, dt=F32):
            return ctx.enter_context(nc.sbuf_tensor(name, shape, dt))

        def sem(name):
            return ctx.enter_context(nc.semaphore(name))

        ident = sb("ident", [128, 128])
        proj_T = sb("proj_T", [128, 4, D])
        w1_hi = sb("w1_hi", [128, E, F], F32R)
        w1_lo = sb("w1_lo", [128, E, F], F32R)
        w3_hi = sb("w3_hi", [128, E, F], F32R)
        w3_lo = sb("w3_lo", [128, E, F], F32R)
        w2_sb = sb("w2_sb", [128, NB, D])
        rw = sb("rw", [128, E])
        b_out_all = sb("b_out_all", [128, D])
        router_b_all = sb("router_b_all", [128, E])
        earlier = sb("earlier", [128, E, E])
        x_in = sb("x_in", [128, C, D])
        xn = sb("xn", [128, C, D])
        xn_T = sb("xn_T", [128, S])
        qk = sb("qk", [128, 2 * S])
        qk_split = sb("qk_split", [128, 2, 2 * S], F32R)
        q_stack = [sb(f"q_stack{i}", [128, H, S], F32R) for i in range(2)]
        k_stack = [sb(f"k_stack{i}", [128, H, S], F32R) for i in range(2)]
        v_pad = [sb(f"v_pad{i}", [128, C, H, 32]) for i in range(2)]
        mx = sb("mx", [128, C, H])
        m_split = sb("m_split", [H // 2, 2, S], F32R)
        w_sq = sb("w_sq", [128, 2, 4 * S])
        poly = sb("poly", [128, U, 4 * S])
        o_T = sb("o_T", [128, G, S])
        den_r = sb("den_r", [128, C, H])
        attn = sb("attn", [128, C, D])
        attn_T = sb("attn_T", [128, S])
        x_res = sb("x_res", [128, C, D])
        x_resb = sb("x_resb", [128, C, D])
        y_acc = [sb(f"y_acc{i}", [128, C, D]) for i in range(2)]
        two = sb("two", [128, 1])
        zero = sb("zero", [128, 1])
        stats = sb("stats", [128, 2 * C, 6])
        mean_var = sb("mean_var", [128, 2 * C, 2])
        eps_all = sb("eps_all", [128, 2 * C])
        minus_half = sb("minus_half", [128, 2 * C])
        three_halves = sb("three_halves", [128, 2 * C])
        half_var = sb("half_var", [128, 2 * C])
        var_eps = sb("var_eps", [128, 2 * C])
        ln_var = sb("ln_var", [128, 2 * C])
        rstd0 = sb("rstd0", [128, 2 * C])
        newton = sb("newton", [128, 2 * C])
        rstd = sb("rstd", [128, 2 * C])
        xn2 = sb("xn2", [128, C, D])
        xn2_T = sb("xn2_T", [128, S])
        xn2_hi = sb("xn2_hi", [128, S], F32R)
        xn2_lo = sb("xn2_lo", [128, S], F32R)
        silu_a = sb("silu_a", [128, 2, 2 * S])
        hid = sb("hid", [128, NB, S])
        logits = sb("logits", [128, C, E])
        top_l = sb("top_l", [128, C])
        shifted = sb("shifted", [128, C, E])
        exp_l = sb("exp_l", [128, C, E])
        above = sb("above", [128, C, E, E])
        equal = sb("equal", [128, C, E, E])
        rank = sb("rank", [128, C, E])
        chosen = sb("chosen", [128, C, E])
        chosen_sum = sb("chosen_sum", [128, C])
        chosen_r = sb("chosen_r", [128, C])
        gates = [sb(f"gates{i}", [128, C, E]) for i in range(2)]

        sc = ctx.enter_context(nc.psum_tensor("sc", [128, 2, 4 * S], F32))
        up_a = ctx.enter_context(nc.psum_tensor("up_a", [128, 2 * S], F32))
        up_b = ctx.enter_context(nc.psum_tensor("up_b", [128, 2 * S], F32))
        pv = ctx.enter_context(nc.psum_tensor("pv", [128, 2, S], F32))
        misc = ctx.enter_context(nc.psum_tensor("misc", [128, 512], F32))

        ld_proj = sem("ld_proj")
        ld_bias = sem("ld_bias")
        ld_experts = sem("ld_experts")
        ident_ok = sem("ident_ok")
        consts_ok = sem("consts_ok")
        consts_v = sem("consts_v")
        blank = [sem(f"blank{i}") for i in range(2)]
        ones_ok = [sem(f"ones_ok{i}") for i in range(2)]
        split_ok = sem("split_ok")
        wT_full = sem("wT_full")
        proj_ok = sem("proj_ok")
        x_loaded = sem("x_loaded")
        xr_loaded = sem("xr_loaded")
        xres_ok = sem("xres_ok")
        agg_ok = sem("agg_ok")
        var_ok = sem("var_ok")
        lnv_ok = sem("lnv_ok")
        rstd0_ok = sem("rstd0_ok")
        newton_step = sem("newton_step")
        rstd_ok = sem("rstd_ok")
        xn_ok = sem("xn_ok")
        xn2_ok = sem("xn2_ok")
        xnT_full = sem("xnT_full")
        xnT_ok = sem("xnT_ok")
        qk_full = sem("qk_full")
        qk_out = sem("qk_out")
        qk_hi_ok = sem("qk_hi_ok")
        qk_ok = sem("qk_ok")
        v_full = sem("v_full")
        v_ok = sem("v_ok")
        qk_stored = sem("qk_stored")
        stacked = [sem(f"stacked{i}") for i in range(2)]
        s_full = sem("s_full")
        s_used = sem("s_used")
        mT_full = sem("mT_full")
        m_hi_ok = sem("m_hi_ok")
        m_ok = sem("m_ok")
        m_stacked = [[sem(f"m_stacked{h}{i}") for i in range(2)] for h in range(2)]
        w_full = sem("w_full")
        sq_ok = sem("sq_ok")
        poly_ok = sem("poly_ok")
        ln_ok = sem("ln_ok")
        p_ok = sem("p_ok")
        pv_full = sem("pv_full")
        o_ok0 = sem("o_ok0")
        o_ok1 = sem("o_ok1")
        oq_full = sem("oq_full")
        den_ok = sem("den_ok")
        attn_ok = sem("attn_ok")
        attnT_full = sem("attnT_full")
        attnT_ok = sem("attnT_ok")
        res_full = sem("res_full")
        y_ok = sem("y_ok")
        xn2T_full = sem("xn2T_full")
        xn2_out = sem("xn2_out")
        xn2_hi_ok = sem("xn2_hi_ok")
        xn2_lo_ok = sem("xn2_lo_ok")
        lg_full = sem("lg_full")
        lg_ok = sem("lg_ok")
        shift_ok = sem("shift_ok")
        exp_ok = sem("exp_ok")
        top_ok = sem("top_ok")
        compared = sem("compared")
        rank_step = sem("rank_step")
        gates_ok = sem("gates_ok")
        a_full = sem("a_full")
        silu_ok = sem("silu_ok")
        b_full = sem("b_full")
        hid_ok = sem("hid_ok")
        down_full = sem("down_full")
        acc_ok = sem("acc_ok")
        stored = [sem(f"stored{i}") for i in range(2)]

        RANK = 2 + E.bit_length() - 1
        GATE = 4

        def no(i, off):
            return 2 * i + off

        def has(i, off):
            return not isinstance(i, int) or 0 <= no(i, off) < B

        def after(eng, s, count):
            if not isinstance(count, int) or count > 0:
                eng.wait_ge(s, count)

        def pair_count(i, off, each):
            return (i + off // 2 + 1) * each

        def over_batches(eng, half_a, half_b):
            for n in range(-2, 4):
                half_a(n // 2, n % 2)
                half_b(n // 2, n % 2)
            with eng.Fori(2, B // 2 - 1) as i:
                for off in range(2):
                    half_a(i, off)
                    half_b(i, off)
            for n in range(B - 2, B + 2):
                half_a(n // 2, n % 2)
                half_b(n // 2, n % 2)

        def blank_q(eng, par):
            eng.memset(q_stack[par][0:MROW].bitcast(F32), 0.0).then_inc(blank[par], 1)

        def blank_k(eng, par):
            eng.memset(k_stack[par][0:MROW].bitcast(F32), 0.0).then_inc(blank[par], 1)

        def blank_k_ones(eng, par):
            eng.memset(k_stack[par][MROW:KROWS].bitcast(F32), 1.0).then_inc(ones_ok[par], 1)

        block = ctx.enter_context(nc.Block())

        @block.sync
        def _(sp):
            sp.dma_start(poly[:, 4, 0:3 * D].rearrange("p (s d) -> p s d", s=3),
                         w_qkv.rearrange("(s o) d -> o s d", s=3)).then_inc(ld_proj, 16)
            sp.dma_start(poly[:, 4, 3 * D:4 * D], w_out).then_inc(ld_proj, 16)

            def other_weights():
                sp.dma_start(b_out_all[:], row_to_all(b_out, D)).then_inc(ld_bias, 16)
                sp.dma_start(router_b_all[:], row_to_all(router_b, E)).then_inc(ld_bias, 16)
                sp.dma_start(rw[:], router_w).then_inc(ld_bias, 16)
                sp.dma_start(poly[:, 0:2, :].rearrange("p a (b f) -> p (a b) f", b=2),
                             w1.rearrange("e d f -> d e f")).then_inc(ld_experts, 16)
                sp.dma_start(poly[:, 2:4, :].rearrange("p a (b f) -> p (a b) f", b=2),
                             w3.rearrange("e d f -> d e f")).then_inc(ld_experts, 16)
                sp.dma_start(w2_sb[:], w2.rearrange("e (c p) d -> p (e c) d", p=128)).then_inc(ld_experts, 16)

            def value(v):
                if not isinstance(v, int):
                    sp.compute_val(v)
                return v

            def address(offset):
                value(offset)
                value(offset * 4)
                return offset

            def batch_at(t, offset):
                return bass.AP(t.tensor, offset, [[D, 128], [128 * D, C], [1, D]])

            def first_half(i, off):
                n = no(i, off)
                par = (off + 1) % 2
                xn_used, x_from, y_from = value(n + 2), address((n + 2) * S * D), address(n * S * D)
                split, scratch_read, w_used = value(n + 2), value(pair_count(i, off, 128)), value(U * n)
                stored_qk, res_used = value(16 * (n + 2)), value(n)
                if has(i, off + 2):
                    after(sp, xn_ok, xn_used)
                    sp.dma_start(x_in[:], batch_at(x, x_from)).then_inc(x_loaded, 16)
                if isinstance(i, int) and n == -2:
                    other_weights()
                if has(i, off + 1):
                    after(sp, qk_ok, split)
                    after(sp, stacked[1 - par], scratch_read)
                    sp.dma_start(scratch.rearrange("a p t -> p a t"),
                                 qk_split[:].rearrange("p a t -> p (a t)").rearrange(
                                     "p (a t) -> p a t", t=S).bitcast(F32)).then_inc(qk_stored, 16)
                    after(sp, w_full, w_used)
                    sp.wait_ge(qk_stored, stored_qk)
                    if isinstance(i, int) and 0 <= n + 1 < 2:
                        sp.wait_ge(blank[par], 2)
                        sp.wait_ge(ones_ok[par], 1)
                    for stack, parts in ((q_stack, (0, 0, 2, 2)), (k_stack, (1, 3, 1, 3))):
                        for r, part in enumerate(parts):
                            sp.dma_start(stack[par][HD * r:HD * (r + 1), :, :].bitcast(F32),
                                         scratch[part].rearrange("(h d) t -> d h t", d=HD)).then_inc(stacked[par], 16)
                if has(i, off):
                    after(sp, xres_ok, res_used)
                    sp.dma_start(x_res[:], batch_at(x, y_from)).then_inc(xr_loaded, 16)

            def second_half(i, off):
                n = no(i, off)
                m_split_at = [value(2 * (n + 1) + h + 1) for h in range(2)]
                added, out_at = value(E * C * (n - 1)), address((n - 2) * S * D)
                if has(i, off + 1):
                    par = (off + 1) % 2
                    for h in range(2):
                        heads = slice(h * H // 2, (h + 1) * H // 2)
                        sp.wait_ge(m_ok, m_split_at[h])
                        for a in range(2):
                            sp.dma_start(q_stack[par][MROW + a:MROW + a + 1, heads, :].bitcast(F32),
                                         m_split[:, a, :].bitcast(F32)).then_inc(m_stacked[h][par], 16)
                if has(i, off - 2):
                    par = off % 2
                    sp.wait_ge(acc_ok, added)
                    sp.dma_start(batch_at(out, out_at), y_acc[par][:]).then_inc(stored[par], 16)

            over_batches(sp, first_half, second_half)
            for par in range(2):
                sp.wait_ge(stored[par], 16 * (B // 2))

        @block.gpsimd
        def _(pool):
            nc.gpsimd.memset(ident[:], 0.0).then_inc(consts_ok, 1)
            nc.gpsimd.memset(earlier[:], 1.0).then_inc(consts_ok, 1)
            nc.gpsimd.memset(eps_all[:], EPS)
            nc.gpsimd.memset(minus_half[:], -0.5)
            nc.gpsimd.memset(zero[:], 0.0)
            nc.gpsimd.memset(three_halves[:], 1.5).then_inc(consts_ok, 1)
            pool.wait_ge(consts_ok, 3)
            nc.gpsimd.affine_select(out=ident[:], in_=ident[:], compare_op=ALU.not_equal, fill=1.0, base=0,
                                    pattern=[[-1, 128]], channel_multiplier=1).then_inc(ident_ok, 1)
            nc.gpsimd.affine_select(out=earlier[:], in_=earlier[:], compare_op=ALU.is_ge, fill=0.0, base=-1,
                                    pattern=[[1, E], [-1, E]], channel_multiplier=0).then_inc(consts_ok, 1)
            pool.wait_ge(consts_ok, 4)
            blank_k_ones(pool, 0)
            pool.wait_ge(ones_ok[0], 1)

            def first_half(i, off):
                if has(i, off + 1):
                    m = no(i, off) + 1
                    pool.wait_ge(qk_out, m + 1)
                    after(pool, qk_stored, 16 * m)
                    nc.gpsimd.tensor_tensor(qk_split[:, 0, :], qk[:], zero[:].to_broadcast([128, 2 * S]),
                                            ALU.add).then_inc(qk_hi_ok, 1)
                    pool.wait_ge(qk_hi_ok, m + 1)
                    nc.gpsimd.tensor_tensor(qk_split[:, 1, :], qk[:], qk_split[:, 0, :].bitcast(F32),
                                            ALU.subtract).then_inc(qk_ok, 1)
                if isinstance(i, int) and no(i, off) == -1:
                    blank_q(pool, 1)
                    blank_k(pool, 1)
                    pool.wait_ge(blank[1], 2)
                    blank_k_ones(pool, 1)
                    pool.wait_ge(ones_ok[1], 1)
                if isinstance(i, int) and no(i, off) == 0:
                    pool.wait_ge(ld_bias, 16 * 3)
                if has(i, off):
                    m = no(i, off)
                    pool.wait_ge(xr_loaded, 16 * (m + 1))
                    after(pool, y_ok, C * m)
                    for c in range(C):
                        last = nc.gpsimd.tensor_tensor(x_resb[:, c, :], x_res[:, c, :], b_out_all[:], ALU.add)
                    last.then_inc(xres_ok, 1)

            def second_half(i, off):
                lo, hi = (0 if has(i, off - 1) else C), (2 * C if has(i, off + 2) else C)
                if lo < hi:
                    n = no(i, off)
                    k = n + 2
                    s = slice(lo, hi)
                    pool.wait_ge(agg_ok, k + 1)
                    nc.gpsimd.tensor_tensor(var_eps[:, s], mean_var[:, s, 1], eps_all[:, s], ALU.add).then_inc(var_ok, 1)
                    pool.wait_ge(var_ok, k + 1)
                    nc.gpsimd.tensor_tensor(half_var[:, s], var_eps[:, s], minus_half[:, s],
                                            ALU.mult).then_inc(newton_step, 1)
                    pool.wait_ge(rstd0_ok, k + 1)
                    nc.gpsimd.tensor_tensor(newton[:, s], rstd0[:, s], rstd0[:, s], ALU.mult).then_inc(newton_step, 1)
                    pool.wait_ge(newton_step, 4 * k + 2)
                    nc.gpsimd.tensor_tensor(newton[:, s], newton[:, s], half_var[:, s], ALU.mult).then_inc(newton_step, 1)
                    pool.wait_ge(newton_step, 4 * k + 3)
                    nc.gpsimd.tensor_tensor(newton[:, s], newton[:, s], three_halves[:, s],
                                            ALU.add).then_inc(newton_step, 1)
                    pool.wait_ge(newton_step, 4 * k + 4)
                    if has(i, off - 1):
                        after(pool, xn2T_full, n - 1)
                    if has(i, off + 2):
                        after(pool, xnT_full, n + 2)
                    nc.gpsimd.tensor_tensor(rstd[:, s], rstd0[:, s], newton[:, s], ALU.mult).then_inc(rstd_ok, 1)
                    nc.gpsimd.drain()
                    for t in range(lo, hi):
                        dst, src = ((xn2[:, t, :], y_acc[(off - 1) % 2][:, t, :]) if t < C
                                    else (xn[:, t - C, :], x_in[:, t - C, :]))
                        ins = nc.gpsimd.tensor_scalar(dst, src, mean_var[:, t, 0:1], rstd[:, t:t + 1], ALU.subtract,
                                                      ALU.mult)
                        if t == C - 1:
                            ins.then_inc(xn2_ok, 1)
                        if t == 2 * C - 1:
                            ins.then_inc(xn_ok, 1)
                if has(i, off - 1):
                    m = no(i, off) - 1
                    pool.wait_ge(xn2_out, m + 1)
                    after(pool, b_full, UP * m)
                    nc.gpsimd.tensor_tensor(xn2_hi[:], xn2_T[:], zero[:].to_broadcast([128, S]),
                                            ALU.add).then_inc(xn2_hi_ok, 1)
                    pool.wait_ge(xn2_hi_ok, m + 1)
                    nc.gpsimd.tensor_tensor(xn2_lo[:], xn2_T[:], xn2_hi[:].bitcast(F32),
                                            ALU.subtract).then_inc(xn2_lo_ok, 1)
                    pool.wait_ge(compared, m + 1)
                    for c in range(C):
                        last = nc.gpsimd.tensor_tensor(equal[:, c], equal[:, c], earlier[:], ALU.mult)
                    last.then_inc(rank_step, 1)
                    pool.wait_ge(rank_step, RANK * m + 1)
                    nc.gpsimd.tensor_tensor(above[:].rearrange("p c i j -> p (c i j)"),
                                            above[:].rearrange("p c i j -> p (c i j)"),
                                            equal[:].rearrange("p c i j -> p (c i j)"),
                                            ALU.add).then_inc(rank_step, 1)
                    j, step = E // 2, 2
                    while j:
                        pool.wait_ge(rank_step, RANK * m + step)
                        dst = above[:, :, :, 0:j] if j > 1 else rank[:].unsqueeze(3)
                        nc.gpsimd.tensor_tensor(dst, above[:, :, :, 0:j], above[:, :, :, j:2 * j],
                                                ALU.add).then_inc(rank_step, 1)
                        j, step = j // 2, step + 1

            over_batches(pool, first_half, second_half)

        @block.scalar
        def _(act):
            def first_half(i, off):
                n = no(i, off)
                act.preload_act_table_set("silu_and_others")

                def square(u):
                    k = U * n + u
                    act.wait_ge(w_full, k + 1)
                    after(act, poly_ok, k - 1 if u > 1 else k - u)
                    nc.scalar.activation(w_sq[:, u % 2, :], sc[:, u % 2, :], ACT.Square).then_inc(sq_ok, 1)

                for u in range(U):
                    if 1 < u < U - 1 and has(i, off):
                        square(u)
                    if u == 2 and has(i, off + 1):
                        m, par = n + 1, (off + 1) % 2
                        act.wait_ge(v_full, m + 1)
                        act.wait_ge(consts_v, 4)
                        after(act, pv_full, G * (m - 1))
                        for c in range(C):
                            last = nc.scalar.copy(v_pad[par][:, c, :, 0:HD],
                                                  pv[:, 0, c * D:(c + 1) * D].rearrange("p (h d) -> p h d", d=HD))
                        last.then_inc(v_ok, 1)
                    if u == 5 and has(i, off - 1):
                        m = n - 1
                        act.wait_ge(attnT_full, m + 1)
                        after(act, res_full, m)
                        nc.scalar.copy(attn_T[:], misc[:, 0:S]).then_inc(attnT_ok, 1)
                    if has(i, off - 2):
                        k = UP * (n - 2) + u
                        act.wait_ge(a_full, k + 1)
                        after(act, hid_ok, k - 1 if u > 1 else k - u)
                        nc.scalar.activation(silu_a[:, u % 2, :], up_a[:], ACT.Silu).then_inc(silu_ok, 1)
                    if u == U - 1 and has(i, off):
                        square(u)
                    if u == 0 and has(i, off):
                        square(0)
                        square(1)
                    if u == 0 and has(i, off + 1):
                        m = n + 1
                        act.wait_ge(qk_full, m + 1)
                        after(act, qk_ok, m)
                        nc.scalar.copy(qk[:], misc[:]).then_inc(qk_out, 1)

            def second_half(i, off):
                n = no(i, off)
                act.preload_act_table_set("natural_log_exp_and_others")

                def log_of(g):
                    act.wait_ge(poly_ok, U * n + C * (g + 1))
                    nc.scalar.activation(poly[:, C * g:C * (g + 1), :], poly[:, C * g:C * (g + 1), :], ACT.Ln,
                                         bias=two[:]).then_inc(ln_ok, 1)

                def weights_of(g):
                    act.wait_ge(ln_ok, G * n + g + 1)
                    nc.scalar.activation(poly[:, C * g:C * (g + 1), :], poly[:, C * g:C * (g + 1), :], ACT.Exp,
                                         scale=-1.0).then_inc(p_ok, 1)

                if has(i, off):
                    log_of(0)
                    log_of(1)
                lo, hi = (0 if has(i, off - 1) else C), (2 * C if has(i, off + 2) else C)
                if lo < hi:
                    k = n + 2
                    s = slice(lo, hi)
                    act.wait_ge(var_ok, k + 1)
                    nc.scalar.activation(ln_var[:, s], var_eps[:, s], ACT.Ln).then_inc(lnv_ok, 1)
                    act.wait_ge(lnv_ok, k + 1)
                    after(act, rstd_ok, k)
                    nc.scalar.activation(rstd0[:, s], ln_var[:, s], ACT.Exp, scale=-0.5).then_inc(rstd0_ok, 1)
                for g in range(G):
                    if has(i, off):
                        if 0 < g < G - 1:
                            log_of(g + 1)
                        weights_of(g)
                    if g == 1 and has(i, off - 1):
                        m = n - 1
                        act.wait_ge(xn2T_full, m + 1)
                        after(act, xn2_lo_ok, m)
                        after(act, lg_full, m)
                        nc.scalar.copy(xn2_T[:], misc[:, 0:S]).then_inc(xn2_out, 1)
                if has(i, off - 1):
                    m = n - 1
                    act.wait_ge(shift_ok, m + 1)
                    after(act, gates_ok, GATE * m)
                    nc.scalar.activation(exp_l[:], shifted[:], ACT.Exp).then_inc(exp_ok, 1)

            act.wait_ge(consts_v, 4)
            over_batches(act, first_half, second_half)

        @block.vector
        def _(dve):
            nc.vector.memset(two[:], 2.0).then_inc(consts_v, 1)
            for par in range(2):
                nc.vector.memset(v_pad[par][:], 0.0)
            nc.vector.memset(gates[0][:], 0.0).then_inc(consts_v, 1)
            dve.wait_ge(consts_v, 2)
            for par in range(2):
                nc.vector.memset(v_pad[par][:, :, :, HD], 1.0).then_inc(consts_v, 1)
            dve.wait_ge(wT_full, 1)
            by_part = misc[:].rearrange("p (s d) -> p s d", s=4)
            for part, factor in ((0, 1.0), (1, -SCALE), (2, 1.0), (3, 1.0)):
                nc.vector.tensor_scalar(proj_T[:, part, :], by_part[:, part, :], factor, None,
                                        ALU.mult).then_inc(proj_ok, 1)

            def split_weights(k, hi, lo, raw):
                nc.vector.tensor_copy(hi, raw).then_inc(split_ok, 1)
                dve.wait_ge(split_ok, 2 * k + 1)
                nc.vector.tensor_tensor(lo, raw, hi.bitcast(F32), ALU.subtract).then_inc(split_ok, 1)

            def split_w1():
                dve.wait_ge(ld_experts, 16 * 3)
                split_weights(0, w1_hi[:].rearrange("p e f -> p (e f)"), w1_lo[:].rearrange("p e f -> p (e f)"),
                              poly[:, 0:2, :].rearrange("p a n -> p (a n)"))

            def split_w3():
                split_weights(1, w3_hi[:].rearrange("p e f -> p (e f)"), w3_lo[:].rearrange("p e f -> p (e f)"),
                              poly[:, 2:4, :].rearrange("p a n -> p (a n)"))

            def first_half(i, off):
                n = no(i, off)
                if isinstance(i, int) and n == -1:
                    blank_q(dve, 0)

                def hidden(u):
                    k = UP * (n - 2) + u
                    dve.wait_ge(b_full, k + 1)
                    dve.wait_ge(silu_ok, k + 1)
                    if u == 0:
                        after(dve, down_full, E * (n - 2))
                    nc.vector.tensor_tensor(hid[:, 2 * u:2 * u + 2, :].rearrange("p a t -> p (a t)"),
                                            silu_a[:, u % 2, :], up_b[:], ALU.mult).then_inc(hid_ok, 1)

                def polynomial(u):
                    k = U * n + u
                    dve.wait_ge(sq_ok, k + 1)
                    if u % C == 0:
                        after(dve, pv_full, G * (n - 1) + u // C + 1)
                    nc.vector.scalar_tensor_tensor(poly[:, u, :], w_sq[:, u % 2, :], 3.0, sc[:, u % 2, :],
                                                   ALU.add, ALU.mult).then_inc(poly_ok, 1)

                def gate_step(k):
                    m, par = n - 2, off % 2
                    if k == 0:
                        dve.wait_ge(rank_step, RANK * (m + 1))
                        dve.wait_ge(exp_ok, m + 1)
                        op = nc.vector.scalar_tensor_tensor(chosen[:], rank[:], 1.5, exp_l[:], ALU.is_lt, ALU.mult)
                    if k == 1:
                        dve.wait_ge(gates_ok, GATE * m + 1)
                        op = nc.vector.tensor_reduce(chosen_sum[:], chosen[:], AX.X, ALU.add)
                    if k == 2:
                        dve.wait_ge(gates_ok, GATE * m + 2)
                        op = nc.vector.reciprocal(chosen_r[:], chosen_sum[:])
                    if k == 3:
                        dve.wait_ge(gates_ok, GATE * m + 3)
                        op = nc.vector.tensor_tensor(gates[par][:], chosen[:],
                                                     chosen_r[:].unsqueeze(2).to_broadcast([128, C, E]), ALU.mult)
                    op.then_inc(gates_ok, 1)

                if has(i, off - 1):
                    dve.wait_ge(pv_full, G * n)
                    after(dve, oq_full, C * (n - 1))
                    nc.vector.tensor_copy(o_T[:, 2:4, :], pv[:]).then_inc(o_ok1, 1)
                if has(i, off + 1):
                    m = n + 1
                    dve.wait_ge(xnT_full, m + 1)
                    after(dve, v_full, m)
                    nc.vector.tensor_copy(xn_T[:], misc[:, 0:S]).then_inc(xnT_ok, 1)
                if isinstance(i, int) and n == -1:
                    dve.wait_ge(ld_bias, 16 * 3)
                if isinstance(i, int) and n == -1:
                    blank_k(dve, 0)
                if isinstance(i, int) and n == 0:
                    split_w3()
                for u in range(U):
                    if has(i, off - 2):
                        hidden(u)
                    if has(i, off):
                        polynomial(u)
                    if u in (1, 2, 3, 4) and has(i, off - 2):
                        gate_step(u - 1)
                    if u in (2, 3) and has(i, off - 1):
                        m, c = n - 1, u - 2
                        by_head = (misc[:] if c == 0 else pv[:].rearrange("p a t -> p (a t)")).rearrange(
                            "p (h e) -> p h e", e=32)
                        dve.wait_ge(oq_full, C * m + c + 1)
                        nc.vector.reciprocal(den_r[:, c, :], by_head[:, :, HD]).then_inc(den_ok, 1)
                        dve.wait_ge(den_ok, C * m + c + 1)
                        after(dve, attnT_full, m)
                        nc.vector.tensor_tensor(attn[:, c, :].rearrange("p (h d) -> p h d", d=HD),
                                                by_head[:, :, 0:HD],
                                                den_r[:, c, :].unsqueeze(2).to_broadcast([128, H, HD]),
                                                ALU.mult).then_inc(attn_ok, 1)
                    if u == 4 and has(i, off + 2):
                        dve.wait_ge(x_loaded, 16 * (n + 3))
                        for c in range(C):
                            nc.vector.bn_stats(stats[:, C + c, :], x_in[:, c, :])
                    if u == 6 and has(i, off - 1):
                        m, par = n - 1, (off - 1) % 2
                        dve.wait_ge(res_full, m + 1)
                        dve.wait_ge(xres_ok, m + 1)
                        after(dve, stored[par], pair_count(i, off - 3, 16))
                        for c in range(C):
                            nc.vector.tensor_tensor(y_acc[par][:, c, :], misc[:, c * D:(c + 1) * D],
                                                    x_resb[:, c, :], ALU.add).then_inc(y_ok, 1)
                if isinstance(i, int) and n == -1:
                    split_w1()

            def second_half(i, off):
                n = no(i, off)
                def statistics():
                    lo, hi = (0 if has(i, off - 1) else C), (2 * C if has(i, off + 2) else C)
                    k = n + 2
                    if lo < hi:
                        if has(i, off - 1):
                            dve.wait_ge(y_ok, C * n)
                        after(dve, xn_ok, min(n + 2, B) if isinstance(i, int) else n + 2)
                        after(dve, xn2_ok, n - 1)
                        for c in range(C if has(i, off - 1) else 0):
                            nc.vector.bn_stats(stats[:, c, :], y_acc[(off - 1) % 2][:, c, :])
                        nc.vector.drain()
                        for s in range(lo, hi):
                            last = nc.vector.bn_aggr(mean_var[:, s, :], stats[:, s, :])
                        last.then_inc(agg_ok, 1)

                def scores_max(u):
                    g, c = u // C, u % C
                    dve.wait_ge(s_full, U * (n + 1) + u + 1)
                    if u == 0:
                        after(dve, mT_full, 2 * (n + 1))
                    nc.vector.tensor_reduce(mx[:, c, 4 * g:4 * g + 4],
                                            sc[:, u % 2, :].rearrange("p (j t) -> p j t", j=4), AX.X, ALU.min,
                                            negate=True).then_inc(s_used, 1)

                def add_expert(e):
                    m, par = n - 2, off % 2
                    dve.wait_ge(down_full, E * m + e + 1)
                    bank = (up_a, up_b)[e % 2]
                    for c in range(C):
                        after(dve, acc_ok, E * C * m + C * e - (C - 1) + c if e else 0)
                        nc.vector.scalar_tensor_tensor(y_acc[par][:, c, :], bank[:, c * D:(c + 1) * D],
                                                       gates[par][:, c, e:e + 1], y_acc[par][:, c, :], ALU.mult,
                                                       ALU.add).then_inc(acc_ok, 1)

                def route_logits():
                    m = n - 1
                    dve.wait_ge(lg_full, m + 1)
                    after(dve, gates_ok, GATE * m)
                    for c in range(C):
                        last = nc.vector.tensor_tensor(logits[:, c, :], misc[:, c * E:(c + 1) * E], router_b_all[:],
                                                       ALU.add)
                    last.then_inc(lg_ok, 1)
                    dve.wait_ge(lg_ok, m + 1)
                    nc.vector.tensor_reduce(top_l[:], logits[:], AX.X, ALU.max).then_inc(top_ok, 1)
                    dve.wait_ge(top_ok, m + 1)
                    after(dve, exp_ok, m)
                    nc.vector.tensor_tensor(shifted[:], logits[:], top_l[:].unsqueeze(2).to_broadcast([128, C, E]),
                                            ALU.subtract).then_inc(shift_ok, 1)

                def split_maxima(h):
                    m = n + 1
                    dve.wait_ge(mT_full, 2 * m + h + 1)
                    after(dve, m_stacked[1 - h][(off + h) % 2], pair_count(i, off + h, 32))
                    nc.vector.tensor_scalar(m_split[:, 0, :], misc[0:H // 2, 0:S], 1.0, None,
                                            ALU.add).then_inc(m_hi_ok, 1)
                    dve.wait_ge(m_hi_ok, 2 * m + h + 1)
                    nc.vector.scalar_tensor_tensor(m_split[:, 1, :], misc[0:H // 2, 0:S], 1.0,
                                                   m_split[:, 0, :].bitcast(F32), ALU.add,
                                                   ALU.subtract).then_inc(m_ok, 1)

                for u in range(U):
                    if has(i, off + 1):
                        scores_max(u)
                    if u == 0:
                        statistics()
                    if u == 6 and has(i, off + 1):
                        split_maxima(0)
                    if u == 7 and has(i, off):
                        dve.wait_ge(pv_full, G * n + 2)
                        after(dve, oq_full, C * n)
                        nc.vector.tensor_copy(o_T[:, 0:2, :], pv[:]).then_inc(o_ok0, 1)
                    if u == 7 and has(i, off - 1):
                        route_logits()
                    if u in (1, 2, 4, 7) and has(i, off - 2):
                        if u == 1:
                            after(dve, gates_ok, GATE * (n - 1))
                        add_expert((1, 2, 4, 7).index(u))
                if has(i, off - 1):
                    for c in range(C):
                        l_j = logits[:, c, :].unsqueeze(1).to_broadcast([128, E, E])
                        l_i = logits[:, c, :].unsqueeze(2).to_broadcast([128, E, E])
                        nc.vector.tensor_tensor(above[:, c], l_j, l_i, ALU.is_gt)
                        last = nc.vector.tensor_tensor(equal[:, c], l_j, l_i, ALU.is_equal)
                    last.then_inc(compared, 1)
                if has(i, off + 1):
                    split_maxima(1)

            dve.wait_ge(consts_ok, 4)
            over_batches(dve, first_half, second_half)

        @block.tensor
        def _(pe):
            pe.wait_ge(ident_ok, 1)
            pe.wait_ge(ld_proj, 16 * 2)
            for s in range(4):
                last = nc.tensor.transpose(misc[:, s * D:(s + 1) * D], poly[:, 4, s * D:(s + 1) * D], ident[:])
            last.then_inc(wT_full, 1)
            pe.wait_ge(proj_ok, 4)

            def exact(dst, lhs, rhs):
                terms = ((0, 0), (0, 1), (1, 0))
                for k, (a, b) in enumerate(terms):
                    last = nc.tensor.matmul(dst, lhs[a], rhs[b], start=(k == 0), stop=(k == len(terms) - 1))
                return last

            def weighted_values(i, off, g):
                n, par = no(i, off), off % 2
                pe.wait_ge(p_ok, G * n + g + 1)
                if g == 0:
                    pe.wait_ge(v_ok, n + 2 if has(i, off + 1) else n + 1)
                    after(pe, attn_ok, C * n)
                if g == 2:
                    pe.wait_ge(o_ok0, n + 1)
                for c in range(C):
                    for j in range(4):
                        last = nc.tensor.matmul(pv[32 * j:32 * j + 32, g % 2, :], v_pad[par][:, c, 4 * g + j, :],
                                                poly[:, C * g + c, j * S:(j + 1) * S], start=(c == 0),
                                                stop=(c == C - 1))
                last.then_inc(pv_full, 1)

            def up(u, dst, hi, lo, full):
                for half in range(2):
                    e, f = divmod(2 * u + half, FB)
                    fs = slice(f * 128, (f + 1) * 128)
                    last = exact(dst[:, half * S:(half + 1) * S], (hi[:, e, fs], lo[:, e, fs]),
                                 (xn2_hi[:], xn2_lo[:]))
                last.then_inc(full, 1)

            def up_a_unit(i, off, u):
                m = no(i, off)
                after(pe, silu_ok, UP * m + u)
                if u == 0:
                    after(pe, acc_ok, E * C * m - C)
                    pe.wait_ge(xn2_lo_ok, m + 1)
                up(u, up_a, w1_hi, w1_lo, a_full)

            def up_b_unit(i, off, u):
                m = no(i, off)
                after(pe, hid_ok, UP * m + u)
                if u == 0:
                    after(pe, acc_ok, E * C * m)
                up(u, up_b, w3_hi, w3_lo, b_full)

            oq = (misc, pv[:].rearrange("p a t -> p (a t)"))

            def distances(i, off, u):
                m, par = no(i, off), off % 2
                g, c = u // C, u % C
                if u < 2:
                    pe.wait_ge(s_used, U * (m + 1) - 1 + u)
                else:
                    pe.wait_ge(poly_ok, U * m + u - 1)
                if u % (U // 2) == 0:
                    pe.wait_ge(m_stacked[u // (U // 2)][par], pair_count(i, off, 32))
                for j in range(4):
                    last = nc.tensor.matmul(sc[:, u % 2, j * S:(j + 1) * S],
                                            k_stack[par][0:KROWS, 4 * g + j, c * 128:(c + 1) * 128],
                                            q_stack[par][0:KROWS, 4 * g + j, :], start=True, stop=True)
                last.then_inc(w_full, 1)

            def first_half(i, off):
                n = no(i, off)
                if has(i, off - 1):
                    weighted_values(i, off - 1, 3)
                if has(i, off + 1):
                    m = n + 1
                    pe.wait_ge(xn_ok, m + 1)
                    if has(i, off):
                        pe.wait_ge(m_ok, 2 * (n + 1))
                    for c in range(C):
                        last = nc.tensor.transpose(misc[:, c * 128:(c + 1) * 128], xn[:, c, :], ident[:])
                    last.then_inc(xnT_full, 1)
                if has(i, off):
                    distances(i, off, 0)
                for u in range(1, U):
                    if u < U - 1 and has(i, off):
                        distances(i, off, u)
                    if u == 1 and has(i, off + 1):
                        m = n + 1
                        pe.wait_ge(xnT_ok, m + 1)
                        nc.tensor.matmul(misc[:, 0:S], proj_T[:, 0, :], xn_T[:], start=True, stop=True)
                        nc.tensor.matmul(misc[:, S:2 * S], proj_T[:, 1, :], xn_T[:], start=True,
                                         stop=True).then_inc(qk_full, 1)
                    if u == 2 and has(i, off + 1):
                        m = n + 1
                        after(pe, o_ok1, n)
                        for c in range(C):
                            last = nc.tensor.matmul(pv[:, 0, c * D:(c + 1) * D], xn_T[:, c * 128:(c + 1) * 128],
                                                    proj_T[:, 2, :], start=True, stop=True)
                        last.then_inc(v_full, 1)
                    if u == 5 and has(i, off - 1):
                        m = n - 1
                        pe.wait_ge(attn_ok, C * (m + 1))
                        for c in range(C):
                            last = nc.tensor.transpose(misc[:, c * 128:(c + 1) * 128], attn[:, c, :], ident[:])
                        last.then_inc(attnT_full, 1)
                    if u == 6 and has(i, off - 1):
                        m = n - 1
                        pe.wait_ge(attnT_ok, m + 1)
                        for c in range(C):
                            last = nc.tensor.matmul(misc[:, c * D:(c + 1) * D], attn_T[:, c * 128:(c + 1) * 128],
                                                    proj_T[:, 3, :], start=True, stop=True)
                        last.then_inc(res_full, 1)
                    if has(i, off - 2):
                        up_a_unit(i, off - 2, u)
                    if u == U - 1 and has(i, off):
                        distances(i, off, u)
                    if has(i, off - 2):
                        up_b_unit(i, off - 2, u)
                    if u in (2, 3) and has(i, off - 1):
                        m, c = n - 1, u - 2
                        if c == 0:
                            pe.wait_ge(o_ok1, m + 1)
                            pe.wait_ge(o_ok0, m + 1)
                            if has(i, off + 1):
                                pe.wait_ge(qk_out, n + 2)
                            else:
                                pe.wait_ge(lg_ok, m)
                                if has(i, off):
                                    pe.wait_ge(m_ok, 2 * (n + 1))
                        elif has(i, off + 1):
                            pe.wait_ge(v_ok, n + 2)
                        for g in range(G):
                            last = nc.tensor.transpose(oq[c][:, g * 128:(g + 1) * 128],
                                                       o_T[:, g, c * 128:(c + 1) * 128], ident[:])
                        last.then_inc(oq_full, 1)

            def second_half(i, off):
                n = no(i, off)
                if isinstance(i, int) and n == 0:
                    pe.wait_ge(split_ok, 4)
                    pe.wait_ge(ld_experts, 16 * 3)
                    pe.wait_ge(ld_bias, 16 * 3)

                def scores(u):
                    m, par = n + 1, (off + 1) % 2
                    g, c = u // C, u % C
                    if u < 2:
                        after(pe, poly_ok, U * m - 1 + u)
                        if u == 0:
                            pe.wait_ge(stacked[par], pair_count(i, off + 1, 128))
                    else:
                        pe.wait_ge(s_used, U * m + u - 1)
                    for j in range(4):
                        last = nc.tensor.matmul(sc[:, u % 2, j * S:(j + 1) * S],
                                                q_stack[par][0:MROW, 4 * g + j, c * 128:(c + 1) * 128],
                                                k_stack[par][0:MROW, 4 * g + j, :], start=True, stop=True)
                    last.then_inc(s_full, 1)

                def down(e):
                    m = n - 2
                    bank = (up_a, up_b)[e % 2]
                    if e == 0:
                        pe.wait_ge(silu_ok, UP * (m + 1))
                        pe.wait_ge(hid_ok, UP * m + 2)
                    if e == 1:
                        pe.wait_ge(hid_ok, UP * (m + 1))
                    if e >= 2:
                        pe.wait_ge(acc_ok, E * C * m + C * (e - 1))
                    for c in range(C):
                        for f in range(FB):
                            last = nc.tensor.matmul(bank[:, c * D:(c + 1) * D],
                                                    hid[:, FB * e + f, c * 128:(c + 1) * 128],
                                                    w2_sb[:, FB * e + f, :], start=(f == 0), stop=(f == FB - 1))
                    last.then_inc(down_full, 1)

                def maxima_T(h):
                    pe.wait_ge(s_used, U * (n + 1) + (h + 1) * U // 2)
                    if h == 0:
                        pe.wait_ge(qk_out, n + 2)
                        after(pe, xn2_out, n)
                    elif has(i, off - 1):
                        pe.wait_ge(lg_ok, n)
                    else:
                        pe.wait_ge(m_ok, 2 * (n + 1) + 1)
                    for c in range(C):
                        last = nc.tensor.transpose(misc[0:H // 2, c * 128:(c + 1) * 128],
                                                   mx[:, c, h * H // 2:(h + 1) * H // 2], ident[:])
                    last.then_inc(mT_full, 1)

                def router_operand():
                    m = n - 1
                    pe.wait_ge(xn2_ok, m + 1)
                    pe.wait_ge(y_ok, C * (m + 1))
                    for c in range(C):
                        last = nc.tensor.transpose(misc[:, c * 128:(c + 1) * 128], xn2[:, c, :], ident[:])
                    last.then_inc(xn2T_full, 1)

                def router_logits():
                    m = n - 1
                    pe.wait_ge(xn2_out, m + 1)
                    if has(i, off + 1):
                        pe.wait_ge(m_ok, 2 * (n + 1) + 1)
                    for c in range(C):
                        cs = slice(c * 128, (c + 1) * 128)
                        last = nc.tensor.matmul(misc[:, c * E:(c + 1) * E], xn2_T[:, cs], rw[:], start=True, stop=True)
                    last.then_inc(lg_full, 1)

                for u in range(U):
                    if has(i, off + 1):
                        scores(u)
                    if u == 0 and has(i, off - 2):
                        down(0)
                    if u == 1 and has(i, off - 2):
                        down(1)
                    if u == 3 and has(i, off - 2):
                        down(2)
                    if u == 4 and has(i, off):
                        weighted_values(i, off, 0)
                    if u == 4 and has(i, off - 1):
                        router_operand()
                    if u == 6 and has(i, off - 2):
                        down(3)
                    if u == 6 and has(i, off + 1):
                        maxima_T(0)
                if has(i, off):
                    weighted_values(i, off, 1)
                if has(i, off - 1):
                    router_logits()
                if has(i, off - 1):
                    up_a_unit(i, off - 1, 0)
                if has(i, off + 1):
                    maxima_T(1)
                if has(i, off):
                    weighted_values(i, off, 2)
                if has(i, off - 1):
                    up_b_unit(i, off - 1, 0)

            over_batches(pe, first_half, second_half)


_INS = ['L0_attn_x', 'L0_attn_w_qkv', 'L0_attn_w_out', 'L0_attn_b_out', 'L0_ffn_router_w', 'L0_ffn_router_b',
        'L0_ffn_w1', 'L0_ffn_w3', 'L0_ffn_w2']
_OUTS = [((32, 256, 128), 'float32')]


def kernel(**inputs):
    import numpy as _np
    import concourse.bacc as _bacc
    from concourse import mybir as _mybir
    from concourse.bass_utils import run_bass_kernel_spmd as _run

    nc = _bacc.Bacc("TRN2", target_bir_lowering=False, num_devices=1)
    arrays, args = {}, []
    for name in _INS:
        a = _np.ascontiguousarray(inputs[name])
        arrays[f"in_{name}_dram"] = a
        args.append(nc.dram_tensor(f"in_{name}_dram", a.shape, _mybir.dt.from_np(a.dtype), kind="ExternalInput").ap())
    for i, (shape, dtype) in enumerate(_OUTS):
        dt = _mybir.dt.from_np(_np.dtype(dtype))
        args.append(nc.dram_tensor(f"out_{i}_dram", shape, dt, kind="ExternalOutput").ap())
    attention_then_experts_kernel(nc, *args)
    r = _run(nc, [arrays], core_ids=[0])
    got = tuple(r.results[0][f"out_{i}_dram"] for i in range(len(_OUTS)))
    return got[0]
```
